# Optimizing a Trainium2 kernel written in Bass

```python
import numpy as np
import jax
import jax.numpy as jnp

def _softmax(x, axis=-1):
    return jax.nn.softmax(x, axis=axis)

def _gelu(x):
    return jax.nn.gelu(x, approximate=True)

def _silu(x):
    return jax.nn.silu(x)

def _sigmoid(x):
    return jax.nn.sigmoid(x)

def _layernorm(x, axis=-1, eps=1e-05):
    m = jnp.mean(x, axis=axis, keepdims=True)
    v = jnp.var(x, axis=axis, keepdims=True)
    return (x - m) / jnp.sqrt(v + eps)

def _scatter_add(tgt, idx, src, axis=0):
    return tgt.at[idx].add(src)

def _segment_sum(src, seg, n):
    return jax.ops.segment_sum(src, seg, n)
kernel_name = 'mk_adj_ffn_d1_adj_r2_cf4da2'

def setup_inputs(seed: int=0):
    np.random.seed(seed)
    _w = jnp.asarray

    def _rec_inputs():
        import jax
        import jax.numpy as jnp
        _gk = jax.random.key(seed)
        x = -0.000929 + 1 * jax.random.normal(jax.random.fold_in(_gk, 1), (64, 128, 128), jnp.float32)
        _w = (1.0 + jnp.arange(128, dtype=jnp.float32)) ** (-0.5)
        _w = _w / _w.mean()
        _pij = jnp.clip(0.125 * _w[:, None] * _w[None, :], 0.0, 1.0)
        _a = jax.random.uniform(jax.random.fold_in(_gk, 2), (64, 128, 128)) < _pij
        _a = jnp.logical_or(_a, jnp.eye(128, dtype=bool))
        _af = _a.astype(jnp.float32)
        adj = _af
        return (x, adj)
    x, adj = _rec_inputs()

    def _L0_gnn_setup():
        import jax, jax.numpy as jnp
        import numpy as np
        B, N = (1, 2048)
        D_IN, D_OUT, H = (128, 128, 8)
        HD = D_OUT // H
        NEG = -9000000000000000.0

        def _xavier(key, shape):
            lim = np.sqrt(6.0 / (shape[0] + shape[1])).astype(np.float32)
            return jax.random.uniform(key, shape, jnp.float32, -lim, lim)
        key = jax.random.key(seed)
        ks = jax.random.split(key, 8)
        x = jax.random.normal(ks[0], (B, N, D_IN), jnp.float32)
        adj = (jax.random.uniform(ks[1], (B, N, N)) < 0.05).astype(jnp.float32)
        idx = jnp.arange(N)
        adj = adj.at[:, idx, idx].set(1.0)
        Wq = _xavier(ks[2], (D_IN, D_OUT))
        bq = jnp.zeros((D_OUT,), jnp.float32)
        Wk = _xavier(ks[3], (D_IN, D_OUT))
        bk = jnp.zeros((D_OUT,), jnp.float32)
        Wv = _xavier(ks[4], (D_IN, D_OUT))
        bv = jnp.zeros((D_OUT,), jnp.float32)
        Wo = _xavier(ks[5], (D_OUT, D_OUT))
        bo = jnp.zeros((D_OUT,), jnp.float32)
        return dict(x=x, adj=adj, Wq=Wq, bq=bq, Wk=Wk, bk=bk, Wv=Wv, bv=bv, Wo=Wo, bo=bo)
    _L0_gnn_all = _L0_gnn_setup()
    _L0_gnn_in = {k: v for k, v in _L0_gnn_all.items() if k in ('Wq', 'bq', 'Wk', 'bk', 'Wv', 'bv', 'Wo', 'bo')}
    del _L0_gnn_all

    def _L0_ffn_setup():
        import jax, jax.numpy as jnp
        import numpy as np
        D_MODEL = 128
        N_EXPERTS = 16
        HIDDEN = 256
        SCALE = 0.02
        key = jax.random.key(seed)
        ks = jax.random.split(key, 5)
        x = jax.random.normal(ks[0], (4, 4096, D_MODEL), dtype=jnp.float32)
        gate_w = jax.random.normal(ks[1], (D_MODEL, N_EXPERTS), dtype=jnp.float32) * SCALE
        gate_b = jnp.zeros((N_EXPERTS,), dtype=jnp.float32)
        w1 = jax.random.normal(ks[2], (N_EXPERTS, D_MODEL, HIDDEN), dtype=jnp.float32) * SCALE
        w2 = jax.random.normal(ks[3], (N_EXPERTS, D_MODEL, HIDDEN), dtype=jnp.float32) * SCALE
        w3 = jax.random.normal(ks[4], (N_EXPERTS, HIDDEN, D_MODEL), dtype=jnp.float32) * SCALE
        return {'x': x, 'gate_w': gate_w, 'gate_b': gate_b, 'w1': w1, 'w2': w2, 'w3': w3}
    _L0_ffn_all = _L0_ffn_setup()
    _L0_ffn_in = {k: v for k, v in _L0_ffn_all.items() if k in ('gate_w', 'gate_b', 'w1', 'w2', 'w3')}
    del _L0_ffn_all
    return {'x': x, 'adj': adj, 'L0_gnn_Wq': _L0_gnn_in['Wq'], 'L0_gnn_bq': _L0_gnn_in['bq'], 'L0_gnn_Wk': _L0_gnn_in['Wk'], 'L0_gnn_bk': _L0_gnn_in['bk'], 'L0_gnn_Wv': _L0_gnn_in['Wv'], 'L0_gnn_bv': _L0_gnn_in['bv'], 'L0_gnn_Wo': _L0_gnn_in['Wo'], 'L0_gnn_bo': _L0_gnn_in['bo'], 'L0_ffn_gate_w': _L0_ffn_in['gate_w'], 'L0_ffn_gate_b': _L0_ffn_in['gate_b'], 'L0_ffn_w1': _L0_ffn_in['w1'], 'L0_ffn_w2': _L0_ffn_in['w2'], 'L0_ffn_w3': _L0_ffn_in['w3']}

def reference(x, adj, L0_gnn_Wq, L0_gnn_bq, L0_gnn_Wk, L0_gnn_bk, L0_gnn_Wv, L0_gnn_bv, L0_gnn_Wo, L0_gnn_bo, L0_ffn_gate_w, L0_ffn_gate_b, L0_ffn_w1, L0_ffn_w2, L0_ffn_w3):
    import jax
    import jax.numpy as jnp

    def _L0_gnn_ref(x, adj, Wq, bq, Wk, bk, Wv, bv, Wo, bo):
        import jax, jax.numpy as jnp
        import numpy as np
        B, N = (1, 2048)
        D_IN, D_OUT, H = (128, 128, 8)
        HD = D_OUT // H
        NEG = -9000000000000000.0

        def _xavier(key, shape):
            lim = np.sqrt(6.0 / (shape[0] + shape[1])).astype(np.float32)
            return jax.random.uniform(key, shape, jnp.float32, -lim, lim)
        b, n, _ = x.shape

        def split_heads(t):
            return t.reshape(b, n, H, HD).transpose(0, 2, 1, 3)
        q = split_heads(x @ Wq + bq)
        k = split_heads(x @ Wk + bk)
        v = split_heads(x @ Wv + bv)
        scores = jnp.einsum('bhqd,bhkd->bhqk', q, k) / np.float32(np.sqrt(HD))
        scores = jnp.where(adj[:, None, :, :] > 0, scores, jnp.float32(NEG))
        attn = jax.nn.softmax(scores, axis=-1)
        out = jnp.einsum('bhqk,bhkd->bhqd', attn, v)
        out = out.transpose(0, 2, 1, 3).reshape(b, n, D_OUT)
        return out @ Wo + bo

    def _L0_ffn_ref(x, gate_w, gate_b, w1, w2, w3):
        import jax, jax.numpy as jnp
        import numpy as np
        D_MODEL = 128
        N_EXPERTS = 16
        HIDDEN = 256
        SCALE = 0.02
        n_experts = w1.shape[0]
        logits = jnp.einsum('bsd,de->bse', x, gate_w) + gate_b
        probs = jax.nn.softmax(logits, axis=-1)
        top_probs, top_idx = jax.lax.top_k(probs, 2)
        top_probs = top_probs / jnp.sum(top_probs, axis=-1, keepdims=True)
        dispatch = jnp.sum(jax.nn.one_hot(top_idx, n_experts, dtype=x.dtype) * top_probs[..., None], axis=-2)
        h1 = jnp.einsum('bsd,edh->bseh', x, w1)
        h2 = jnp.einsum('bsd,edh->bseh', x, w2)
        hidden = jax.nn.silu(h1) * h2
        expert_out = jnp.einsum('bseh,eho->bseo', hidden, w3)
        return jnp.einsum('bseo,bse->bso', expert_out, dispatch)
    x = x + _L0_gnn_ref(_layernorm(x, axis=-1), adj, L0_gnn_Wq, L0_gnn_bq, L0_gnn_Wk, L0_gnn_bk, L0_gnn_Wv, L0_gnn_bv, L0_gnn_Wo, L0_gnn_bo)
    x = x + _L0_ffn_ref(_layernorm(x, axis=-1), L0_ffn_gate_w, L0_ffn_gate_b, L0_ffn_w1, L0_ffn_w2, L0_ffn_w3)
    return x

_drawn_inputs = setup_inputs


def setup_inputs(seed=0):
    import zlib

    import numpy as np

    out = dict(_drawn_inputs(seed))
    spreads = {'L0_gnn_bq': (0.0, 0.295),
     'L0_gnn_bk': (0.0, 0.8),
     'L0_gnn_bv': (0.0, 0.1),
     'L0_gnn_bo': (0.0, 0.1),
     'L0_ffn_gate_b': (0.0, 0.8)}
    factors = {'L0_ffn_gate_w': 8.0, 'L0_ffn_w1': 8.0, 'L0_ffn_w2': 8.0, 'L0_ffn_w3': 8.0}
    for name, (base, spread) in spreads.items():
        noise = np.random.default_rng([zlib.crc32(name.encode()), seed]).standard_normal(out[name].shape)
        drawn = base * np.exp(spread * noise) if base else spread * noise
        out[name] = jnp.asarray(drawn.astype(out[name].dtype))
    for name, factor in factors.items():
        out[name] = (out[name] * factor).astype(out[name].dtype)
    return out
```

```python
from contextlib import ExitStack

import concourse.bass as bass
from concourse import mybir

F32 = mybir.dt.float32
BF16 = mybir.dt.bfloat16
I32 = mybir.dt.int32
U32 = mybir.dt.uint32
ALU = mybir.AluOpType
ACT = mybir.ActivationFunctionType
AX = mybir.AxisListType

P = 128
EPS = 1e-5
NEG = -9000000000000000.0
QUAD = 4


def static(v):
    return isinstance(v, int)


def wait(eng, sem, count):
    if not static(count) or count > 0:
        eng.wait_ge(sem, count)


def graph_attention_moe(nc, x, adj, wq, bq, wk, bk, wv, bv, wo, bo, gate_w, gate_b, w1, w2, w3, out):
    G, N, D = x.shape
    E, _, HID = w1.shape
    HEADS = 8
    HD = D // HEADS
    assert N == P and D == P and HID == 2 * P and HD == 16 and G % QUAD == 0
    QSCALE = float(HD) ** -0.5
    TOKENS = G * N
    TOPK = 2
    REGION = TOKENS + P
    ROW = D + 2
    NT_MAX = TOPK * TOKENS // P + E - 1
    NT = -(-NT_MAX // 8) * 8
    FILL_ROW = E * REGION
    CHUNK = 4
    RING = 8
    PAIRS = 8
    NCHUNK = G // CHUNK
    X_FIRST = min(3 * CHUNK, G)

    STATS, APPLY, XT, QKV = 5, 4, 3, 2
    T_FIRST = -STATS
    T_LOOP = 14
    T_LOOP_END = T_LOOP + (G - STATS - T_LOOP) // QUAD * QUAD
    T_LAST = G - QUAD + 12
    assert T_LOOP_END > T_LOOP

    xs = nc.dram_tensor("slots", (E * REGION + P, ROW), F32, kind="Internal").ap()
    ys = nc.dram_tensor("expert_rows", (TOPK * TOKENS, D), F32, kind="Internal").ap()

    with ExitStack() as ctx:
        def sb(name, shape, dt=F32):
            return ctx.enter_context(nc.sbuf_tensor(name, shape, dt))

        def sem(name):
            return ctx.enter_context(nc.semaphore(name))

        bank = [ctx.enter_context(nc.psum_tensor(f"bank{i}", [P, 512], F32)) for i in range(8)]
        score_bank, pt_bank, misc_bank = bank[0:4], bank[4:6], bank[6:8]

        x_all = sb("x_all", [P, G * D])
        adj_all = sb("adj_all", [P, G * N])
        x2n_all = adj_all
        w12_sb = sb("w12_sb", [P, E * 2 * HID])
        w3_sb = sb("w3_sb", [P, E * 2 * D])
        wq_sb, wk_sb, wv_sb, wo_sb = (sb(n, [P, D]) for n in ("wq_sb", "wk_sb", "wv_sb", "wo_sb"))
        gw_sb = sb("gw_sb", [P, E])
        bv_bc, bo_bc, gb_bc = sb("bv_bc", [P, D]), sb("bo_bc", [P, D]), sb("gb_bc", [P, E])
        bqk = sb("bqk", [P, 2])
        ident, neg_ident = sb("ident", [P, P]), sb("neg_ident", [P, P], BF16)
        before_bf, ones_bf = sb("before_bf", [P, P], BF16), sb("ones_bf", [P, P], BF16)
        head_of = sb("head_of", [P, HEADS])
        parity, bk_parity, bq_scaled = sb("parity", [P, 2]), sb("bk_parity", [P, 2]), sb("bq_scaled", [P, 1])
        neg_half = sb("neg_half", [P, 1])
        expert_iota, region_base = sb("expert_iota", [P, E]), sb("region_base", [P, E])
        stats1, mv1, rstd1 = sb("stats1", [P, 2, 6]), sb("mv1", [P, 2, 2]), sb("rstd1", [P, 2, 2])
        stats2, mv2, rstd2 = sb("stats2", [P, 2, 6]), sb("mv2", [P, 2, 2]), sb("rstd2", [P, 2, 2])
        xn, xnT = sb("xn", [P, 2, D]), sb("xnT", [P, 2, P])
        qT, k_par = sb("qT", [P, 2, P]), sb("k_par", [P, 2, 2, P])
        v_aug = sb("v_aug", [P, 4, HEADS, HD + 1])
        no_edge = sb("no_edge", [P, G * N], BF16)
        neg_max = sb("neg_max", [P, 2, HEADS])
        probs, probsT = sb("probs", [P, 2, HEADS, P]), sb("probsT", [P, HEADS, P])
        recip_sum, o_norm, o_T = sb("recip_sum", [P, HEADS]), sb("o_norm", [P, D]), sb("o_T", [P, P])
        x2n, x2T = sb("x2n", [P, 4, D]), sb("x2T", [P, P])
        logits = sb("logits", [P, QUAD, E])
        top_val, top_idx = sb("top_val", [P, QUAD, 8]), sb("top_idx", [P, QUAD, 8], U32)
        top_f = sb("top_f", [P, QUAD * TOPK])
        onehot, chosen = sb("onehot", [P, QUAD, TOPK, E]), sb("chosen", [P, QUAD, E], BF16)
        gap, gap_exp, gap_den = sb("gap", [P, QUAD]), sb("gap_exp", [P, QUAD]), sb("gap_den", [P, QUAD])
        gates = sb("gates", [P, QUAD, TOPK])
        next_free = sb("next_free", [P, E])
        place, place_hot = sb("place", [P, QUAD, E]), sb("place_hot", [P, QUAD, TOPK, E])
        slot = sb("slot", [P, QUAD, TOPK], I32)
        slot_out = sb("slot_out", [P, QUAD, TOPK], I32)
        dest = sb("dest", [P, QUAD, TOPK])
        rows = sb("rows", [P, QUAD, TOPK, ROW])
        counts, next_free_i = sb("counts", [P, E]), sb("next_free_i", [P, E], I32)
        one = sb("one", [P, 1])
        upto16, tile_iota, tile_row0 = sb("upto16", [E, E]), sb("tile_iota", [E, NT]), sb("tile_row0", [1, NT])
        ntiles_a, ntiles_i = sb("ntiles_a", [E, 1], I32), sb("ntiles_i", [E, 1], I32)
        ntiles, tiles_upto, jump = sb("ntiles", [E, 1]), sb("tiles_upto", [E, 1]), sb("jump", [E, 1])
        passed = sb("passed", [E, NT])
        expert_f, row_f = sb("expert_f", [1, NT]), sb("row_f", [1, NT])
        w12_at, w3_at, row_at = (sb(n, [1, NT], I32) for n in ("w12_at", "w3_at", "row_at"))
        fill = sb("fill", [P, ROW])
        tile_in = sb("tile_in", [P, RING, ROW])
        tile_T = sb("tile_T", [P, 2, P])
        silu, hidden, hiddenT = sb("silu", [P, 2, HID]), sb("hidden", [P, 2, HID]), sb("hiddenT", [P, 2, HID])
        tile_out = sb("tile_out", [P, RING, D])
        pair_rows = w12_sb[:, 0:PAIRS * CHUNK * TOPK * D].rearrange("p (r g d) -> p r g d", r=PAIRS, g=CHUNK)
        pair_sum = x2n_all[:, 0:2 * CHUNK * D].rearrange("p (r g d) -> p r g d", r=2, g=CHUNK)

        s = {n: sem(n) for n in (
            "small_loaded", "x_first_loaded", "x_rest_loaded", "adj_first_loaded", "adj_rest_loaded", "experts_loaded",
            "const_zeroed", "const_made", "const_dve", "const_dve2",
            "stats1_done", "mv1_done", "var1_eps", "rstd1_done", "xn_done", "xT_psum", "xnT_done",
            "qkv_psum", "qk_done", "v_done", "mask_done", "score_psum", "max_done", "exp_done",
            "pt_psum", "pt0_done", "pt1_done", "pv_psum", "recip_done", "o_done", "oT_psum", "oT_done",
            "wo_psum", "x2_done", "x_bo_done", "stats2_done", "mv2_done", "var2_eps", "rstd2_done", "x2n_done", "x2n_kept",
            "x2T_psum", "x2T_done", "logit_psum", "logit_done",
            "top_val_done", "top_idx_done", "top_f_done", "onehot_done", "chosen_done", "gap_done", "gap_exp_done",
            "rank_psum", "place_done", "free_done", "place_hot_done", "slot_done", "gap_den_done", "gate1_done",
            "gates_done", "rows_made", "dest_done",
            "counts_done", "free_i_done", "counts_psum", "nt_a", "nt_i", "nt_f", "upto_psum", "upto_done", "jump_done",
            "passed_done", "table_psum", "table_f", "table_done", "regions_filled",
            "tile_T_psum", "tile_T_done", "gemm1_psum", "silu_done", "hidden_done", "hT_psum", "hT_done",
            "gemm2_psum", "tile_out_done", "sum_done", "out_done", "apart",
        )}
        scattered = [sem(f"scattered{u}") for u in range(QUAD)]
        tile_loaded = [sem(f"tile_loaded{u}") for u in range(RING)]
        tile_scattered = [sem(f"tile_scattered{u}") for u in range(RING)]
        pair_loaded = [sem(f"pair_loaded{u}") for u in range(PAIRS)]

        def wait_apart(eng, semaphore, count):
            wait(eng, semaphore, count)
            eng.sem_inc(s["apart"], 1)

        def cols(tensor, g, width=D):
            return tensor[:, g * width:(g + 1) * width] if static(g) else tensor[:, bass.ds(g * width, width)]

        def live(g):
            return not static(g) or 0 <= g < G

        def upto(count, most=G):
            return min(count, most) if static(count) else count

        def run_steps(eng, step):
            for t in range(T_FIRST, T_LOOP):
                step(t, t % QUAD)
            with eng.Fori(T_LOOP, T_LOOP_END - QUAD + 1, QUAD) as t:
                for k in range(QUAD):
                    step(t + k, (T_LOOP + k) % QUAD)
            for t in range(T_LOOP_END, T_LAST + 1):
                step(t, t % QUAD)

        def run_tiles(eng, tile_step):
            first, last = -1, NT + 2
            start = RING + 2
            end = start + (NT - 1 - start) // RING * RING
            for t in range(first, start):
                tile_step(t, t % RING)
            with eng.Fori(start, end - RING + 1, RING) as t:
                for k in range(RING):
                    tile_step(t + k, (start + k) % RING)
            for t in range(end, last):
                tile_step(t, t % RING)

        def quad_of(t, offset):
            if static(t):
                q = (t - offset) // QUAD
                return q if 0 <= q < G // QUAD else None
            return t

        def quad_count(t, offset, each=1):
            if static(t):
                return each * ((t - offset) // QUAD + 1)
            return (t - (offset - QUAD)) * each // QUAD if each % QUAD else (t - (offset - QUAD)) * (each // QUAD)

        block = ctx.enter_context(nc.Block())

        @block.sync
        def _(sp):
            x_v = x.rearrange("g n d -> n g d")
            adj_v = adj.rearrange("g n m -> n g m")
            xa = x_all[:, :].rearrange("p (g d) -> p g d", d=D)
            aa = adj_all[:, :].rearrange("p (g d) -> p g d", d=N)
            sp.dma_start(xa[:, 0:X_FIRST, :], x_v[:, 0:X_FIRST, :]).then_inc(s["x_first_loaded"], 16)
            for dst, src in ((wq_sb, wq), (wk_sb, wk), (wv_sb, wv), (wo_sb, wo), (gw_sb, gate_w)):
                sp.dma_start(dst[:, :], src).then_inc(s["small_loaded"], 16)
            for j, src in ((0, bq), (1, bk)):
                sp.dma_start(bqk[:, j:j + 1], src.rearrange("(p a) -> p a", a=1)).then_inc(s["small_loaded"], 16)
            for dst, src in ((bv_bc, bv), (bo_bc, bo), (gb_bc, gate_b)):
                sp.dma_start(dst[:, :], src.rearrange("(a d) -> a d", a=1).to_broadcast([P, dst.shape[1]])
                             ).then_inc(s["small_loaded"], 16)
            sp.dma_start(aa[:, 0:X_FIRST, :], adj_v[:, 0:X_FIRST, :]).then_inc(s["adj_first_loaded"], 16)
            sp.dma_start(xa[:, X_FIRST:G, :], x_v[:, X_FIRST:G, :]).then_inc(s["x_rest_loaded"], 16)
            sp.dma_start(aa[:, X_FIRST:G, :], adj_v[:, X_FIRST:G, :]).then_inc(s["adj_rest_loaded"], 16)
            w12_v = w12_sb[:, :].rearrange("p (e a h) -> p e a h", e=E, a=2)
            sp.dma_start(w12_v[:, :, 0, :], w1.rearrange("e d h -> d e h")).then_inc(s["experts_loaded"], 16)
            sp.dma_start(w12_v[:, :, 1, :], w2.rearrange("e d h -> d e h")).then_inc(s["experts_loaded"], 16)
            w3_v = w3_sb[:, :].rearrange("p (e c d) -> p e c d", e=E, c=2)
            for e in range(E):
                sp.dma_start(w3_v[:, e, :, :], w3[e].rearrange("(c p) o -> p c o", p=P)).then_inc(s["experts_loaded"], 16)

            sp.wait_ge(s["free_i_done"], 1)
            for e in range(E):
                first = sp.value_load(next_free_i[0:1, e:e + 1], min_val=e * REGION, max_val=e * REGION + TOKENS)
                sp.dma_start(xs[bass.ds(first, P), :], fill[:, :]).then_inc(s["regions_filled"], 16)
            sp.dma_start(xs[FILL_ROW:FILL_ROW + P, :], fill[:, :]).then_inc(s["regions_filled"], 16)

            for u in range(QUAD):
                sp.wait_ge(scattered[u], 16 * TOPK * (G // QUAD))
            sp.wait_ge(s["regions_filled"], 16 * (E + 1))
            sp.wait_ge(s["table_done"], 3)

            def load_tile(t, u, first_lap):
                if not first_lap:
                    wait_apart(sp, tile_scattered[u], (t - u) * (16 // RING))
                row = sp.value_load(row_at[0:1, bass.ds(t, 1)], min_val=0, max_val=FILL_ROW)
                sp.dma_start(tile_in[:, u, :], xs[bass.ds(row, P), :]).then_inc(tile_loaded[u], 16)

            for t in range(RING):
                load_tile(t, t, True)
            with sp.Fori(RING, NT - RING + 1, RING) as t:
                for k in range(RING):
                    load_tile(t + k, k, False)

            for u in range(RING):
                sp.wait_ge(tile_scattered[u], 16 * (NT // RING))
            ys_v = ys[0:TOPK * TOKENS, :].rearrange("(c g p k) d -> c p g (k d)", g=CHUNK, p=P, k=TOPK)
            out_v = out.rearrange("(c g) n d -> c n g d", g=CHUNK)
            for c in range(min(PAIRS, NCHUNK)):
                sp.dma_start(pair_rows[:, c % PAIRS], ys_v[c]).then_inc(pair_loaded[c % PAIRS], 16)
            for c in range(NCHUNK):
                sp.wait_ge(s["out_done"], c + 1)
                if c + PAIRS < NCHUNK:
                    sp.dma_start(pair_rows[:, c % PAIRS], ys_v[c + PAIRS]).then_inc(pair_loaded[c % PAIRS], 16)
                sp.dma_start(out_v[c], xa[:, c * CHUNK:(c + 1) * CHUNK, :]).then_inc(s["sum_done"], 16)
            sp.wait_ge(s["sum_done"], 16 * NCHUNK)

        @block.gpsimd
        def _(pool):
            g_ = nc.gpsimd
            g_.memset(ident[:, :], 0.0)
            g_.memset(before_bf[:, :], 1.0)
            g_.memset(ones_bf[:, :], 1.0)
            g_.memset(head_of[:, :], 1.0)
            g_.memset(neg_half[:, :], -0.5)
            g_.memset(one[:, :], 1.0)
            g_.memset(upto16[:, :], 1.0)
            g_.memset(v_aug[:, :, :, :], 1.0)
            g_.memset(fill[:, :], 0.0)
            g_.iota(expert_iota[:, :], [[1, E]], base=0, channel_multiplier=0, allow_small_or_imprecise_dtypes=True)
            g_.iota(region_base[:, :], [[REGION // P, E]], base=0, channel_multiplier=0,
                    allow_small_or_imprecise_dtypes=True)
            g_.iota(tile_iota[:, :], [[1, NT]], base=0, channel_multiplier=0, allow_small_or_imprecise_dtypes=True)
            g_.iota(tile_row0[:, :], [[P, NT]], base=0, channel_multiplier=0, allow_small_or_imprecise_dtypes=True)
            g_.iota(dest[:, :, :], [[TOPK * P, QUAD], [1, TOPK]], base=0, channel_multiplier=TOPK,
                    allow_small_or_imprecise_dtypes=True).then_inc(s["const_zeroed"], 1)
            pool.wait_ge(s["const_zeroed"], 1)
            g_.affine_select(out=ident[:, :], in_=ident[:, :], compare_op=ALU.not_equal, fill=1.0, base=0,
                             pattern=[[-1, P]], channel_multiplier=1)
            g_.affine_select(out=before_bf[:, :], in_=before_bf[:, :], compare_op=ALU.is_gt, fill=0.0, base=0,
                             pattern=[[1, P]], channel_multiplier=-1)
            g_.affine_select(out=upto16[:, :], in_=upto16[:, :], compare_op=ALU.is_ge, fill=0.0, base=0,
                             pattern=[[1, E]], channel_multiplier=-1)
            g_.iota(fill[:, D + 1:D + 2].bitcast(I32), [[1, 1]], base=TOPK * TOKENS, channel_multiplier=1)
            g_.tensor_scalar(region_base[:, :], region_base[:, :], float(P), None, ALU.mult)
            g_.affine_select(out=head_of[:, :], in_=head_of[:, :], compare_op=ALU.is_ge, fill=0.0, base=0,
                             pattern=[[-HD, HEADS]], channel_multiplier=1).then_inc(s["const_zeroed"], 1)
            pool.wait_ge(s["const_zeroed"], 2)
            g_.affine_select(out=head_of[:, :], in_=head_of[:, :], compare_op=ALU.is_ge, fill=0.0, base=HD - 1,
                             pattern=[[HD, HEADS]], channel_multiplier=-1).then_inc(s["const_made"], 1)
            pool.wait_ge(s["small_loaded"], 16 * 10)

            def step(t, k):
                g = t + STATS
                if live(g):
                    b = (k + STATS) % 2
                    wait_apart(pool, s["mv1_done"], g + 1)
                    g_.tensor_scalar(rstd1[:, b, 0:1], mv1[:, b, 1:2], EPS, None, ALU.add).then_inc(s["var1_eps"], 1)
                    wait_apart(pool, s["var1_eps"], g + 1)
                    g_.tensor_tensor(rstd1[:, b, 1:2], rstd1[:, b, 0:1], neg_half[:, :], ALU.pow
                                     ).then_inc(s["rstd1_done"], 1)
                g = t + XT
                if live(g):
                    pool.wait_ge(s["xn_done"], g + 1)
                    g_.tensor_tensor(cols(x_all, g), cols(x_all, g), bo_bc[:, :], ALU.add).then_inc(s["x_bo_done"], 1)
                g = t - 2
                if live(g):
                    b = k % 2
                    wait_apart(pool, s["mv2_done"], g + 1)
                    g_.tensor_scalar(rstd2[:, b, 0:1], mv2[:, b, 1:2], EPS, None, ALU.add).then_inc(s["var2_eps"], 1)
                    wait_apart(pool, s["var2_eps"], g + 1)
                    g_.tensor_tensor(rstd2[:, b, 1:2], rstd2[:, b, 0:1], neg_half[:, :], ALU.pow
                                     ).then_inc(s["rstd2_done"], 1)
                g = t - 3
                if live(g):
                    pool.wait_ge(s["x2n_done"], g + 1)
                    g_.tensor_copy(cols(x2n_all, g), x2n[:, (k + 1) % 4, :]).then_inc(s["x2n_kept"], 1)
                offset, us = {2: (10, (0,)), 3: (11, (1,)), 0: (12, (2, 3)), 1: (0, ())}[k]
                if us and quad_of(t, offset) is not None:
                    if k == 2:
                        pool.wait_ge(s["gates_done"], quad_count(t, offset))
                        pool.wait_ge(s["slot_done"], quad_count(t, offset))
                    for u in us:
                        wait(pool, scattered[u], quad_count(t, offset + QUAD, 16 * TOPK))
                        g = t - offset + u if static(t) else t + (u - offset)
                        pool.wait_ge(s["x2n_kept"], g + 1)
                        g_.tensor_copy(rows[:, u, :, 0:D], cols(x2n_all, g).unsqueeze(1).to_broadcast([P, TOPK, D]))
                        g_.tensor_copy(rows[:, u, :, D], gates[:, u, :])
                        g_.tensor_copy(rows[:, u, :, D + 1].bitcast(I32), dest[:, u, :])
                        g_.tensor_copy(slot_out[:, u, :], slot[:, u, :]).then_inc(s["rows_made"], 1)
                        wait_apart(pool, s["rows_made"], g + 1)
                        g_.tensor_scalar(dest[:, u, :], dest[:, u, :], float(QUAD * P * TOPK), None, ALU.add
                                         ).then_inc(s["dest_done"], 1)
                        for c in range(TOPK):
                            g_.indirect_dma_start(
                                out=xs, out_offset=bass.IndirectOffsetOnAxis(ap=slot_out[:, u, c:c + 1], axis=0),
                                in_=rows[:, u, c, :], in_offset=None,
                                bounds_check=FILL_ROW - 1, oob_is_err=False).then_inc(scattered[u], 16)
                        wait_apart(pool, s["dest_done"], g + 1)

            run_steps(pool, step)

            def scatter_tile(t, u):
                wait_apart(pool, s["tile_out_done"], t + 1)
                g_.indirect_dma_start(
                    out=ys, out_offset=bass.IndirectOffsetOnAxis(ap=tile_in[:, u, D + 1:D + 2].bitcast(I32), axis=0),
                    in_=tile_out[:, u, :], in_offset=None,
                    bounds_check=TOPK * TOKENS - 1, oob_is_err=False).then_inc(tile_scattered[u], 16)

            with pool.Fori(0, NT - RING + 1, RING) as t:
                for u in range(RING):
                    scatter_tile(t + u, u)

        @block.vector
        def _(dve):
            v = nc.vector
            dve.wait_ge(s["const_made"], 1)
            dve.wait_ge(s["small_loaded"], 16 * 10)
            v.tensor_scalar(neg_ident[:, :], ident[:, :], NEG, None, ALU.mult)
            v.tensor_copy(next_free[:, :], region_base[:, :])
            v.tensor_scalar(bq_scaled[:, :], bqk[:, 0:1], QSCALE, None, ALU.mult)
            v.tensor_reduce(parity[:, :], head_of[:, :].rearrange("p (j a) -> p a j", a=2), AX.X, ALU.add
                            ).then_inc(s["const_dve"], 1)
            dve.wait_ge(s["const_dve"], 1)
            v.tensor_scalar(bk_parity[:, :], parity[:, :], bqk[:, 1:2], None, ALU.mult).then_inc(s["const_dve2"], 1)
            dve.wait_ge(s["x_first_loaded"], 16)

            def mark_absent(first, last):
                v.tensor_scalar(no_edge[:, first * N:last * N], adj_all[:, first * N:last * N], 0.0, None, ALU.is_le
                                ).then_inc(s["mask_done"], 1)

            def route_top2(t):
                wait_apart(dve, s["logit_done"], t - 4)
                for u in range(QUAD):
                    v.max(top_val[:, u, :], logits[:, u, :]).then_inc(s["top_val_done"], 1)
                for u in range(QUAD):
                    wait_apart(dve, s["top_val_done"], t - 8 + u + 1)
                    v.max_index(top_idx[:, u, :], top_val[:, u, :], logits[:, u, :]).then_inc(s["top_idx_done"], 1)
                v.tensor_tensor(gap[:, :], top_val[:, :, 1], top_val[:, :, 0], ALU.subtract).then_inc(s["gap_done"], 1)
                dve.wait_ge(s["top_idx_done"], t - 4)
                v.tensor_copy(top_f[:, :].rearrange("p (u c) -> p u c", c=TOPK), top_idx[:, :, 0:TOPK]
                              ).then_inc(s["top_f_done"], 1)
                dve.wait_ge(s["top_f_done"], quad_count(t, 8))
                v.tensor_tensor(onehot[:, :, :, :].rearrange("p u c e -> p (u c) e"),
                                expert_iota[:, :].unsqueeze(1).to_broadcast([P, QUAD * TOPK, E]),
                                top_f[:, :].unsqueeze(2).to_broadcast([P, QUAD * TOPK, E]), ALU.is_equal
                                ).then_inc(s["onehot_done"], 1)
                dve.wait_ge(s["onehot_done"], quad_count(t, 8))
                v.tensor_tensor(chosen[:, :, :], onehot[:, :, 0, :], onehot[:, :, 1, :], ALU.add
                                ).then_inc(s["chosen_done"], 1)

            def route_slots(t, misc):
                q = quad_count(t, 9)
                rank = misc[:, 256:256 + (QUAD + 1) * E].rearrange("p (u e) -> p u e", e=E)
                dve.wait_ge(s["rank_psum"], q)
                wait(dve, s["free_done"], quad_count(t, 9 + QUAD))
                v.tensor_tensor(place[:, :, :], rank[:, 0:QUAD, :],
                                next_free[:, :].unsqueeze(1).to_broadcast([P, QUAD, E]), ALU.add
                                ).then_inc(s["place_done"], 1)
                dve.wait_ge(s["place_done"], q)
                v.tensor_tensor(next_free[:, :], rank[:, QUAD, :], next_free[:, :], ALU.add).then_inc(s["free_done"], 1)
                for c in range(TOPK):
                    hot = v.tensor_tensor(place_hot[:, :, c, :], onehot[:, :, c, :], place[:, :, :], ALU.mult)
                hot.then_inc(s["place_hot_done"], 1)
                dve.wait_ge(s["place_hot_done"], q)
                wait(dve, s["rows_made"], (q - 1) * QUAD if static(q) else t - 9)
                with nc.allow_low_precision(reason="whole numbers below 2^24, exact in float32 and int32"):
                    v.tensor_reduce(slot[:, :, :].rearrange("p u c -> p (u c)"),
                                    place_hot[:, :, :, :].rearrange("p u c e -> p (u c) e"), AX.X, ALU.add
                                    ).then_inc(s["slot_done"], 1)
                dve.wait_ge(s["gap_exp_done"], q)
                v.tensor_scalar(gap_den[:, :], gap_exp[:, :], 1.0, None, ALU.add).then_inc(s["gap_den_done"], 1)
                dve.wait_ge(s["gap_den_done"], q)
                v.reciprocal(gates[:, :, 0], gap_den[:, :]).then_inc(s["gate1_done"], 1)
                dve.wait_ge(s["gate1_done"], q)
                v.tensor_tensor(gates[:, :, 1], gates[:, :, 0], gap_exp[:, :], ALU.mult).then_inc(s["gates_done"], 1)

            def step(t, k):
                m0, m1 = misc_bank[k % 2], misc_bank[(k + 1) % 2]
                if static(t) and t == X_FIRST - STATS:
                    dve.wait_ge(s["x_rest_loaded"], 16)
                if static(t) and t == -2:
                    dve.wait_ge(s["adj_first_loaded"], 16)
                    mark_absent(0, X_FIRST)
                if static(t) and t == X_FIRST - 2:
                    dve.wait_ge(s["adj_rest_loaded"], 16)
                    mark_absent(X_FIRST, G)

                def row_max(h):
                    dve.wait_ge(s["score_psum"], 2 * t + h + 1)
                    for j in range(2):
                        mx = v.tensor_reduce(neg_max[:, k % 2, 4 * h + 2 * j:4 * h + 2 * j + 2],
                                             score_bank[2 * h + j][:, 0:2 * P].rearrange("p (a n) -> p a n", a=2),
                                             AX.X, ALU.max, negate=True)
                    mx.then_inc(s["max_done"], 1)

                if live(t):
                    row_max(0)
                g = t - 1
                if live(g):
                    dve.wait_ge(s["pt_psum"], 2 * g + 1)
                    wait(dve, s["pv_psum"], 2 * (g - 1) + 1)
                    v.tensor_copy(probsT[:, 0:4, :], pt_bank[0][:, :].rearrange("p (h n) -> p h n", h=4)
                                  ).then_inc(s["pt0_done"], 1)
                g = t + APPLY
                if live(g):
                    b = (k + APPLY) % 2
                    dve.wait_ge(s["rstd1_done"], g + 1)
                    wait(dve, s["xT_psum"], g - 1)
                    v.tensor_scalar(xn[:, b, :], cols(x_all, g), mv1[:, b, 0:1], rstd1[:, b, 1:2],
                                    ALU.subtract, ALU.mult).then_inc(s["xn_done"], 1)
                g = t - 2
                if live(g):
                    dve.wait_ge(s["wo_psum"], g + 1)
                    dve.wait_ge(s["x_bo_done"], g + 1)
                    v.tensor_tensor(cols(x_all, g), m0[:, 0:D], cols(x_all, g), ALU.add).then_inc(s["x2_done"], 1)
                g = t + STATS
                if live(g):
                    b = (k + STATS) % 2
                    v.bn_stats(stats1[:, b, :], cols(x_all, g)).then_inc(s["stats1_done"], 1)
                    wait_apart(dve, s["stats1_done"], g + 1)
                    v.bn_aggr(mv1[:, b, :], stats1[:, b, :]).then_inc(s["mv1_done"], 1)
                g = t - 2
                if live(g):
                    b = k % 2
                    wait_apart(dve, s["x2_done"], g + 1)
                    v.bn_stats(stats2[:, b, :], cols(x_all, g)).then_inc(s["stats2_done"], 1)
                    wait_apart(dve, s["stats2_done"], g + 1)
                    v.bn_aggr(mv2[:, b, :], stats2[:, b, :]).then_inc(s["mv2_done"], 1)
                if live(t):
                    row_max(1)
                if k == 0 and quad_of(t, 8) is not None:
                    if quad_of(t, 12) is not None:
                        dve.wait_ge(s["slot_done"], quad_count(t, 12))
                    route_top2(t)
                g = t - 4
                if live(g):
                    dve.wait_ge(s["logit_psum"], g + 1)
                    wait(dve, s["x2T_psum"], upto(t - 2))
                    if k == 1 and quad_of(t, 9) is not None:
                        dve.wait_ge(s["rank_psum"], quad_count(t, 9))
                    v.tensor_tensor(logits[:, k, :], m1[:, P:P + E], gb_bc[:, :], ALU.add).then_inc(s["logit_done"], 1)
                g = t - 3
                if live(g):
                    dve.wait_ge(s["x2T_psum"], g + 1)
                    v.tensor_copy(x2T[:, :], m1[:, 0:P]).then_inc(s["x2T_done"], 1)
                if k == 1 and quad_of(t, 9) is not None:
                    route_slots(t, m1)
                g = t - 1
                if live(g):
                    o_ps = m0[:, 0:HEADS * (HD + 1)].rearrange("p (h d) -> p h d", h=HEADS)
                    dve.wait_ge(s["pv_psum"], 2 * g + 2)
                    v.reciprocal(recip_sum[:, :], o_ps[:, :, HD]).then_inc(s["recip_done"], 1)
                    dve.wait_ge(s["recip_done"], g + 1)
                    wait(dve, s["oT_psum"], g)
                    v.tensor_tensor(o_norm[:, :].rearrange("p (h d) -> p h d", h=HEADS), o_ps[:, :, 0:HD],
                                    recip_sum[:, :].unsqueeze(2).to_broadcast([P, HEADS, HD]), ALU.mult
                                    ).then_inc(s["o_done"], 1)
                g = t - 2
                if live(g):
                    b = k % 2
                    dve.wait_ge(s["rstd2_done"], g + 1)
                    wait(dve, s["x2T_psum"], g - 3)
                    wait(dve, s["x2n_kept"], g - 3)
                    v.tensor_scalar(x2n[:, (k + 2) % 4, :], cols(x_all, g), mv2[:, b, 0:1], rstd2[:, b, 1:2],
                                    ALU.subtract, ALU.mult).then_inc(s["x2n_done"], 1)
                g = t + QKV
                if live(g):
                    dve.wait_ge(s["qk_done"], g + 1)
                    wait(dve, s["pv_psum"], 2 * (g - 4) + 2)
                    v.tensor_tensor(v_aug[:, (k + QKV) % 4, :, 0:HD],
                                    m1[:, 2 * P:3 * P].rearrange("p (h d) -> p h d", h=HEADS),
                                    bv_bc[:, :].rearrange("p (h d) -> p h d", h=HEADS), ALU.add
                                    ).then_inc(s["v_done"], 1)

            run_steps(dve, step)

            dve.wait_ge(s["free_done"], G // QUAD)
            v.tensor_copy(next_free_i[:, :], next_free[:, :]).then_inc(s["free_i_done"], 1)
            v.tensor_tensor(counts[:, :], next_free[:, :], region_base[:, :], ALU.subtract).then_inc(s["counts_done"], 1)
            dve.wait_ge(s["counts_psum"], 1)
            v.tensor_scalar(ntiles_a[:, :], misc_bank[0][0:E, 0:1], float(P - 1), None, ALU.add).then_inc(s["nt_a"], 1)
            dve.wait_ge(s["nt_a"], 1)
            v.tensor_scalar(ntiles_i[:, :], ntiles_a[:, :], P.bit_length() - 1, None, ALU.arith_shift_right
                            ).then_inc(s["nt_i"], 1)
            dve.wait_ge(s["nt_i"], 1)
            v.tensor_copy(ntiles[:, :], ntiles_i[:, :]).then_inc(s["nt_f"], 1)
            dve.wait_ge(s["nt_f"], 1)
            v.tensor_scalar(jump[:, :], ntiles[:, :], -float(P), float(REGION), ALU.mult, ALU.add
                            ).then_inc(s["jump_done"], 1)
            dve.wait_ge(s["upto_psum"], 1)
            v.tensor_copy(tiles_upto[:, :], misc_bank[1][0:E, 0:1]).then_inc(s["upto_done"], 1)
            dve.wait_ge(s["upto_done"], 1)
            v.tensor_scalar(passed[:, :], tile_iota[:, :], tiles_upto[:, :], None, ALU.is_ge
                            ).then_inc(s["passed_done"], 1)
            dve.wait_ge(s["table_psum"], 1)
            v.tensor_scalar(expert_f[:, :], misc_bank[0][0:1, 0:NT], float(E - 1), None, ALU.min)
            v.tensor_tensor(row_f[:, :], misc_bank[1][0:1, 0:NT], tile_row0[:, :], ALU.add).then_inc(s["table_f"], 1)
            dve.wait_ge(s["table_f"], 1)
            v.tensor_scalar(w12_at[:, :], expert_f[:, :], float(2 * HID), None, ALU.mult).then_inc(s["table_done"], 1)
            v.tensor_scalar(w3_at[:, :], expert_f[:, :], float(2 * D), None, ALU.mult).then_inc(s["table_done"], 1)
            v.tensor_scalar(row_at[:, :], row_f[:, :], float(FILL_ROW), None, ALU.min).then_inc(s["table_done"], 1)

            def tile_step(t, k):
                if not static(t) or 0 <= t < NT:
                    b = k % 2
                    dve.wait_ge(s["silu_done"], t + 1)
                    wait(dve, s["hT_psum"], t - 1)
                    v.tensor_tensor(hidden[:, b, :], silu[:, b, :], bank[b][:, HID:2 * HID], ALU.mult
                                    ).then_inc(s["hidden_done"], 1)
                g = t - 1
                if not static(g) or 0 <= g < NT:
                    b = (k + 1) % 2
                    dve.wait_ge(s["hT_psum"], g + 1)
                    wait(dve, s["gemm2_psum"], g - 1)
                    v.tensor_copy(hiddenT[:, b, :], bank[2 + b][:, 0:HID]).then_inc(s["hT_done"], 1)

            run_tiles(dve, tile_step)

            for c in range(NCHUNK):
                xc = x_all[:, c * CHUNK * D:(c + 1) * CHUNK * D].rearrange("p (g d) -> p g d", d=D)
                dve.wait_ge(pair_loaded[c % PAIRS], 16 * (c // PAIRS + 1))
                v.tensor_tensor(pair_sum[:, c % 2], pair_rows[:, c % PAIRS, :, 0:D], pair_rows[:, c % PAIRS, :, D:2 * D],
                                ALU.add).then_inc(s["table_f"], 1)
                dve.wait_ge(s["table_f"], c + 2)
                v.tensor_tensor(xc, xc, pair_sum[:, c % 2], ALU.add).then_inc(s["out_done"], 1)

        @block.scalar
        def _(act):
            a = nc.scalar
            act.wait_ge(s["const_dve2"], 1)

            def step(t, k):
                m0, m1 = misc_bank[k % 2], misc_bank[(k + 1) % 2]

                def exps(h):
                    act.wait_ge(s["max_done"], 2 * t + h + 1)
                    wait(act, s["pt_psum"], 2 * (t - 2) + h + 1)
                    for i in range(4):
                        head = 4 * h + i
                        ex = a.activation(probs[:, k % 2, head, :], score_bank[head // 2][:, (head % 2) * P:(head % 2 + 1) * P],
                                          ACT.Exp, bias=neg_max[:, k % 2, head:head + 1])
                    ex.then_inc(s["exp_done"], 1)

                g = t - 2
                if live(g):
                    act.wait_ge(s["oT_psum"], g + 1)
                    a.copy(o_T[:, :], m1[:, 0:P]).then_inc(s["oT_done"], 1)
                if live(t):
                    exps(0)
                g = t - 1
                if live(g):
                    act.wait_ge(s["pt_psum"], 2 * g + 2)
                    wait(act, s["pv_psum"], 2 * (g - 1) + 2)
                    a.copy(probsT[:, 4:8, :], pt_bank[1][:, :].rearrange("p (h n) -> p h n", h=4)
                           ).then_inc(s["pt1_done"], 1)
                g = t + XT
                if live(g):
                    act.wait_ge(s["xT_psum"], g + 1)
                    wait(act, s["qkv_psum"], g - 1)
                    a.copy(xnT[:, (k + XT) % 2, :], m1[:, 0:P]).then_inc(s["xnT_done"], 1)
                if live(t):
                    exps(1)
                if k == 1 and quad_of(t, 9) is not None:
                    q = quad_count(t, 9)
                    act.wait_ge(s["gap_done"], q)
                    wait(act, s["gates_done"], quad_count(t, 9 + QUAD))
                    a.activation(gap_exp[:, :], gap[:, :], ACT.Exp).then_inc(s["gap_exp_done"], 1)
                g = t + QKV
                if live(g):
                    b = (k + QKV) % 2
                    act.wait_ge(s["qkv_psum"], g + 1)
                    a.activation(qT[:, b, :], m1[:, 0:P], ACT.Identity, bias=bq_scaled[:, :], scale=QSCALE)
                    for par in range(2):
                        kk = a.activation(k_par[:, b, par, :], m1[:, P:2 * P], ACT.Identity,
                                          bias=bk_parity[:, par:par + 1], scale=parity[:, par:par + 1])
                    kk.then_inc(s["qk_done"], 1)

            run_steps(act, step)

            def tile_step(t, k):
                if not static(t) or 0 <= t < NT:
                    b = k % 2
                    act.wait_ge(s["gemm1_psum"], t + 1)
                    wait(act, s["hidden_done"], t - 1)
                    a.activation(silu[:, b, :], bank[b][:, 0:HID], ACT.Silu).then_inc(s["silu_done"], 1)
                g = t + 1
                if not static(g) or g < NT:
                    b = (k + 1) % 2
                    act.wait_ge(s["tile_T_psum"], g + 1)
                    wait(act, s["gemm1_psum"], g - 1)
                    a.copy(tile_T[:, b, :], bank[6 + b][:, 0:P]).then_inc(s["tile_T_done"], 1)
                g = t - 2
                if not static(g) or 0 <= g < NT:
                    u = (k - 2) % RING
                    act.wait_ge(s["gemm2_psum"], g + 1)
                    if not static(g) or g >= RING:
                        act.wait_ge(tile_scattered[u], (g - u) * (16 // RING))
                    a.activation(tile_out[:, u, :], bank[4 + k % 2][:, 0:D], ACT.Copy,
                                 scale=tile_in[:, u, D:D + 1]).then_inc(s["tile_out_done"], 1)

            run_tiles(act, tile_step)

        @block.tensor
        def _(pe):
            mm, tr = nc.tensor.matmul, nc.tensor.transpose
            pe.wait_ge(s["const_dve2"], 1)

            def step(t, k):
                m0, m1 = misc_bank[k % 2], misc_bank[(k + 1) % 2]

                def scores(h):
                    wait(pe, s["exp_done"], 2 * (t - 1) + h + 1)
                    for j in range(2 * h, 2 * h + 2):
                        mm(score_bank[j][:, 0:2 * P].rearrange("p (a n) -> p a n", a=2), neg_ident[:, :],
                           cols(no_edge, t).unsqueeze(1).to_broadcast([P, 2, P]), start=True, stop=False)
                        rows32 = slice(32 * j, 32 * j + 32)
                        sc = mm(score_bank[j][:, 0:2 * P], qT[rows32, k % 2, :],
                                k_par[rows32, k % 2, :, :].rearrange("p a n -> p (a n)"), start=False, stop=True)
                    sc.then_inc(s["score_psum"], 1)

                def transpose_probs(h):
                    g = t - 1
                    pe.wait_ge(s["exp_done"], 2 * g + h + 1)
                    wait(pe, s["pt1_done" if h else "pt0_done"], g)
                    for i in range(4):
                        last = tr(pt_bank[h][:, i * P:(i + 1) * P], probs[:, (k + 1) % 2, 4 * h + i, :], ident[:, :])
                    last.then_inc(s["pt_psum"], 1)

                def weigh_values(h):
                    g = t - 1
                    pe.wait_ge(s["pt1_done" if h else "pt0_done"], g + 1)
                    for head in range(4 * h, 4 * h + 4):
                        last = mm(m0[:, head * (HD + 1):(head + 1) * (HD + 1)], probsT[:, head, :],
                                  v_aug[:, (k + 3) % 4, head, :], start=True, stop=True)
                    last.then_inc(s["pv_psum"], 1)

                if live(t):
                    pe.wait_ge(s["qk_done"], t + 1)
                    if static(t):
                        pe.wait_ge(s["mask_done"], 1 if t < X_FIRST else 2)
                    scores(0)
                g = t - 2
                if live(g):
                    pe.wait_ge(s["o_done"], g + 1)
                    tr(m1[:, 0:P], o_norm[:, :], ident[:, :]).then_inc(s["oT_psum"], 1)
                if live(t - 1):
                    transpose_probs(0)
                if live(g):
                    pe.wait_ge(s["oT_done"], g + 1)
                    pe.wait_ge(s["v_done"], upto(t + 2))
                    if static(t):
                        wait(pe, s["x2T_done"], upto(t - 3))
                        wait(pe, s["logit_done"], upto(t - 4))
                        wait(pe, s["free_done"], upto((t - 10) // QUAD + 1, G // QUAD))
                    mm(m0[:, 0:D], o_T[:, :], wo_sb[:, :], start=True, stop=True).then_inc(s["wo_psum"], 1)
                if live(t - 1):
                    transpose_probs(1)
                g = t + XT
                if live(g):
                    pe.wait_ge(s["xn_done"], g + 1)
                    wait(pe, s["oT_done"], t - 1)
                    if static(t):
                        wait(pe, s["v_done"], t + 1)
                    tr(m1[:, 0:P], xn[:, (k + XT) % 2, :], ident[:, :]).then_inc(s["xT_psum"], 1)
                if live(t):
                    scores(1)
                if live(t - 1):
                    wait(pe, s["x2_done"], t - 1)
                    pe.wait_ge(s["v_done"], upto(t + 2))
                    weigh_values(0)
                if live(t - 4) or live(t - 3) or (k == 1 and quad_of(t, 9) is not None):
                    pe.wait_ge(s["xnT_done"], upto(t + XT + 1))
                    if static(t):
                        wait(pe, s["oT_done"], upto(t - 1))
                        wait(pe, s["x2_done"], upto(t - 2))
                        wait(pe, s["logit_done"], upto(t - 5))
                        wait(pe, s["x2T_done"], upto(t - 4))
                if live(t - 4):
                    pe.wait_ge(s["x2T_done"], t - 3)
                    mm(m1[:, P:P + E], x2T[:, :], gw_sb[:, :], start=True, stop=True).then_inc(s["logit_psum"], 1)
                if k == 1 and quad_of(t, 9) is not None:
                    pe.wait_ge(s["chosen_done"], quad_count(t, 9))
                    for u in range(QUAD + 1):
                        at = m1[:, 256 + u * E:256 + (u + 1) * E]
                        if u < QUAD:
                            last = mm(at, before_bf[:, :], chosen[:, u, :], start=True, stop=(u == 0))
                        for w in range(u):
                            last = mm(at, ones_bf[:, :], chosen[:, w, :], start=(u == QUAD and w == 0), stop=(w == u - 1))
                    last.then_inc(s["rank_psum"], 1)
                g = t - 3
                if live(g):
                    pe.wait_ge(s["x2n_done"], g + 1)
                    tr(m1[:, 0:P], x2n[:, (k + 1) % 4, :], ident[:, :]).then_inc(s["x2T_psum"], 1)
                if live(t - 1):
                    weigh_values(1)
                g = t + QKV
                if live(g):
                    b = (k + QKV) % 2
                    pe.wait_ge(s["xnT_done"], upto(g + 2))
                    wait(pe, s["x2T_done"], t - 2)
                    wait(pe, s["logit_done"], t - 3)
                    if k == 1 and quad_of(t, 9) is not None:
                        pe.wait_ge(s["free_done"], quad_count(t, 9))
                    mm(m1[:, 0:P], wq_sb[:, :], xnT[:, b, :], start=True, stop=True)
                    mm(m1[:, P:2 * P], wk_sb[:, :], xnT[:, b, :], start=True, stop=True)
                    mm(m1[:, 2 * P:3 * P], xnT[:, b, :], wv_sb[:, :], start=True, stop=True).then_inc(s["qkv_psum"], 1)

            run_steps(pe, step)

            pe.wait_ge(s["counts_done"], 1)
            mm(misc_bank[0][0:E, 0:1], counts[0:1, :], one[0:1, :], start=True, stop=True).then_inc(s["counts_psum"], 1)
            pe.wait_ge(s["nt_f"], 1)
            mm(misc_bank[1][0:E, 0:1], upto16[:, :], ntiles[:, :], start=True, stop=True).then_inc(s["upto_psum"], 1)
            pe.wait_ge(s["passed_done"], 1)
            pe.wait_ge(s["jump_done"], 1)
            mm(misc_bank[0][0:1, 0:NT], one[0:E, :], passed[:, :], start=True, stop=True)
            mm(misc_bank[1][0:1, 0:NT], jump[:, :], passed[:, :], start=True, stop=True).then_inc(s["table_psum"], 1)
            pe.wait_ge(s["table_done"], 3)
            pe.wait_ge(s["experts_loaded"], 16 * (2 + E))

            def at_tile(table, t, most):
                return pe.value_load(table[0:1, bass.ds(t, 1)] if not static(t) else table[0:1, t:t + 1],
                                     min_val=0, max_val=most)

            def tile_step(t, k):
                if not static(t) or 0 <= t < NT:
                    b = k % 2
                    col = at_tile(w12_at, t, (E - 1) * 2 * HID)
                    pe.wait_ge(s["tile_T_done"], t + 1)
                    wait(pe, s["hidden_done"], t - 1)
                    mm(bank[b][:, :], tile_T[:, b, :], w12_sb[:, bass.ds(col, 2 * HID)], start=True, stop=True
                       ).then_inc(s["gemm1_psum"], 1)
                g = t - 2
                if not static(g) or 0 <= g < NT:
                    b = k % 2
                    pe.wait_ge(s["hT_done"], g + 1)
                    wait(pe, s["tile_out_done"], g - 1)
                    col = at_tile(w3_at, g, (E - 1) * 2 * D)
                    for c in range(2):
                        last = mm(bank[4 + b][:, 0:D], hiddenT[:, b, c * P:(c + 1) * P],
                                  w3_sb[:, bass.ds(col + c * D, D)], start=(c == 0), stop=(c == 1))
                    last.then_inc(s["gemm2_psum"], 1)
                g = t + 1
                if not static(g) or g < NT:
                    b, u = (k + 1) % 2, (k + 1) % RING
                    pe.wait_ge(tile_loaded[u], (g + (RING - u)) * (16 // RING))
                    wait(pe, s["tile_T_done"], g - 1)
                    tr(bank[6 + b][:, 0:P], tile_in[:, u, 0:D], ident[:, :]).then_inc(s["tile_T_psum"], 1)
                g = t - 1
                if not static(g) or 0 <= g < NT:
                    b = (k + 1) % 2
                    pe.wait_ge(s["hidden_done"], g + 1)
                    wait(pe, s["hT_done"], g - 1)
                    for c in range(2):
                        last = tr(bank[2 + b][:, c * P:(c + 1) * P], hidden[:, b, c * P:(c + 1) * P], ident[:, :])
                    last.then_inc(s["hT_psum"], 1)

            run_tiles(pe, tile_step)


_INS = ["x", "adj", "L0_gnn_Wq", "L0_gnn_bq", "L0_gnn_Wk", "L0_gnn_bk", "L0_gnn_Wv", "L0_gnn_bv", "L0_gnn_Wo",
        "L0_gnn_bo", "L0_ffn_gate_w", "L0_ffn_gate_b", "L0_ffn_w1", "L0_ffn_w2", "L0_ffn_w3"]


def kernel(**inputs):
    import numpy as np
    import concourse.bacc as bacc
    from concourse.bass_utils import run_bass_kernel_spmd

    nc = bacc.Bacc("TRN2", target_bir_lowering=False, num_devices=1)
    arrays, args = {}, []
    for name in _INS:
        a = np.ascontiguousarray(inputs[name])
        arrays[f"in_{name}"] = a
        args.append(nc.dram_tensor(f"in_{name}", a.shape, mybir.dt.from_np(a.dtype), kind="ExternalInput").ap())
    out = nc.dram_tensor("out", arrays["in_x"].shape, F32, kind="ExternalOutput").ap()
    graph_attention_moe(nc, *args, out)
    r = run_bass_kernel_spmd(nc, [arrays], core_ids=[0])
    return r.results[0]["out"]
```

```python
from contextlib import ExitStack

import concourse.bass as bass
from concourse import mybir

F32 = mybir.dt.float32
BF16 = mybir.dt.bfloat16
I32 = mybir.dt.int32
U32 = mybir.dt.uint32
ALU = mybir.AluOpType
ACT = mybir.ActivationFunctionType
AX = mybir.AxisListType

P = 128
EPS = 1e-5
NEG = -9000000000000000.0
QUAD = 4


def static(v):
    return isinstance(v, int)


def wait(eng, sem, count):
    if not static(count) or count > 0:
        eng.wait_ge(sem, count)


def graph_attention_moe(nc, x, adj, wq, bq, wk, bk, wv, bv, wo, bo, gate_w, gate_b, w1, w2, w3, out):
    G, N, D = x.shape
    E, _, HID = w1.shape
    HEADS = 8
    HD = D // HEADS
    assert N == P and D == P and HID == 2 * P and HD == 16 and G % QUAD == 0
    QSCALE = float(HD) ** -0.5
    TOKENS = G * N
    TOPK = 2
    REGION = TOKENS + P
    ROW = D + 2
    NT_MAX = TOPK * TOKENS // P + E - 1
    NT = -(-NT_MAX // 8) * 8
    FILL_ROW = E * REGION
    WIDTH = 2 * HID + 2 * D
    CHUNK = 4
    RING = 8
    PAIRS = 8
    TILE_LOOP = RING + 2
    NCHUNK = G // CHUNK
    X_FIRST = min(3 * CHUNK, G)

    STATS, APPLY, XT, QKV = 5, 4, 3, 2
    T_FIRST = -STATS
    T_LOOP = 14
    T_LOOP_END = T_LOOP + (G - STATS - T_LOOP) // QUAD * QUAD
    T_LAST = G - QUAD + 13
    assert T_LOOP_END > T_LOOP

    xs = nc.dram_tensor("slots", (E * REGION + P, ROW), F32, kind="Internal").ap()
    ys = nc.dram_tensor("expert_rows", (TOPK * TOKENS, D), F32, kind="Internal").ap()

    with ExitStack() as ctx:
        def sb(name, shape, dt=F32):
            return ctx.enter_context(nc.sbuf_tensor(name, shape, dt))

        def sem(name):
            return ctx.enter_context(nc.semaphore(name))

        bank = [ctx.enter_context(nc.psum_tensor(f"bank{i}", [P, 512], F32)) for i in range(8)]
        score_bank, pt_bank, misc_bank = bank[0:4], bank[4:6], bank[6:8]

        x_all = sb("x_all", [P, G * D])
        adj_all = sb("adj_all", [P, G * N])
        x2n_all = adj_all
        w_sb = sb("w_sb", [P, E * WIDTH])
        wq_sb, wk_sb, wv_sb, wo_sb = (sb(n, [P, D]) for n in ("wq_sb", "wk_sb", "wv_sb", "wo_sb"))
        gw_sb = sb("gw_sb", [P, E])
        bo_bc, bv_cols, gb_bc = sb("bo_bc", [P, D]), sb("bv_cols", [P, P]), sb("gb_bc", [P, E])
        bqkv = sb("bqkv", [P, 3])
        ident, neg_ident = sb("ident", [P, P]), sb("neg_ident", [P, P], BF16)
        before_bf, ones_bf = sb("before_bf", [P, P], BF16), sb("ones_bf", [P, P], BF16)
        head_of, parity = sb("head_of", [P, HEADS]), sb("parity", [P, 2])
        bk_parity, bq_scaled = sb("bk_parity", [P, 2]), sb("bq_scaled", [P, 1])
        neg_half = sb("neg_half", [P, 2])
        expert_iota, region_base = sb("expert_iota", [P, E]), sb("region_base", [P, E])
        stats, mean_var = sb("stats", [P, 2, 6]), sb("mean_var", [P, 2, 2, 2])
        var_eps, rstd = sb("var_eps", [P, 2, 2]), sb("rstd", [P, 2, 2])
        xn, xnT = sb("xn", [P, 2, D]), sb("xnT", [P, 2, P])
        qT, q_pairs, k_parity = sb("qT", [P, 2, P]), sb("q_pairs", [P, 2, 4, P]), sb("k_parity", [P, 2, 2, P])
        v_aug = sb("v_aug", [P, 4, HEADS, HD + 1])
        no_edge = sb("no_edge", [P, G * N], BF16)
        neg_max = sb("neg_max", [P, 2, HEADS])
        probs, probsT = sb("probs", [P, 2, HEADS, P]), sb("probsT", [P, HEADS, P])
        recip_sum, o_norm, o_T = sb("recip_sum", [P, HEADS]), sb("o_norm", [P, D]), sb("o_T", [P, P])
        x2n, x2T = sb("x2n", [P, 4, D]), sb("x2T", [P, P])
        logits = sb("logits", [P, QUAD, E])
        top_val, top_idx = sb("top_val", [P, QUAD, 8]), sb("top_idx", [P, QUAD, 8], U32)
        top_f = sb("top_f", [P, QUAD * TOPK])
        onehot, chosen = sb("onehot", [P, QUAD, TOPK, E]), sb("chosen", [P, QUAD, E], BF16)
        gap, gap_exp, gap_den = sb("gap", [P, QUAD]), sb("gap_exp", [P, QUAD]), sb("gap_den", [P, QUAD])
        gates = sb("gates", [P, QUAD, TOPK])
        next_free = sb("next_free", [P, E])
        place, place_hot = sb("place", [P, QUAD, E]), sb("place_hot", [P, QUAD, TOPK, E])
        slot = sb("slot", [P, QUAD, TOPK], I32)
        slot_out = sb("slot_out", [P, QUAD, TOPK], I32)
        dest = sb("dest", [P, QUAD, TOPK])
        rows = sb("rows", [P, QUAD, TOPK, ROW])
        counts, next_free_i = sb("counts", [P, E]), sb("next_free_i", [P, E], I32)
        one = sb("one", [P, 1])
        upto16, tile_iota, tile_row0 = sb("upto16", [E, E]), sb("tile_iota", [E, NT]), sb("tile_row0", [1, NT])
        ntiles_a, ntiles_i = sb("ntiles_a", [E, 1], I32), sb("ntiles_i", [E, 1], I32)
        ntiles, tiles_upto, jump = sb("ntiles", [E, 1]), sb("tiles_upto", [E, 1]), sb("jump", [E, 1])
        passed = sb("passed", [E, NT])
        expert_f, row_f = sb("expert_f", [1, NT]), sb("row_f", [1, NT])
        w_at, row_at = (sb(n, [1, NT], I32) for n in ("w_at", "row_at"))
        fill = sb("fill", [P, ROW])
        tile_in = sb("tile_in", [P, RING, ROW])
        tile_T = sb("tile_T", [P, 2, P])
        silu, hidden, hiddenT = sb("silu", [P, 2, HID]), sb("hidden", [P, 2, HID]), sb("hiddenT", [P, 2, HID])
        tile_out = sb("tile_out", [P, RING, D])
        pair_rows = w_sb[:, 0:PAIRS * CHUNK * TOPK * D].rearrange("p (r g d) -> p r g d", r=PAIRS, g=CHUNK)
        pair_sum = x2n_all[:, 0:2 * CHUNK * D].rearrange("p (r g d) -> p r g d", r=2, g=CHUNK)

        s = {n: sem(n) for n in (
            "small_loaded", "x_first_loaded", "x_rest_loaded", "adj_first_loaded", "adj_rest_loaded", "experts_loaded",
            "const_zeroed", "const_made", "const_dve", "parity_done",
            "q_spread", "bias_psum", "bias_done",
            "stats1_done", "mv1_done", "eps_done", "rstd_done", "xn_done", "xT_psum", "xnT_done",
            "qkv_psum", "qkv_done", "mask_done", "score_psum", "max_done", "exp_done",
            "pt_psum", "pt0_done", "pt1_done", "pv_psum", "recip_done", "o_done", "oT_psum", "oT_done",
            "wo_psum", "x2_done", "x_bo_done", "stats2_done", "mv2_done", "x2n_done", "x2n_kept",
            "x2T_psum", "x2T_done", "logit_psum", "logit_done",
            "top_val_done", "top_idx_done", "top_f_done", "onehot_done", "chosen_done", "gap_done", "gap_exp_done",
            "rank_psum", "place_done", "free_done", "place_hot_done", "slot_done", "gap_den_done", "gate1_done",
            "gates_done", "rows_made", "row_data", "dest_done",
            "counts_done", "free_i_done", "counts_psum", "nt_a", "nt_i", "nt_f", "upto_psum", "upto_done", "jump_done",
            "passed_done", "table_psum", "table_f", "table_done", "regions_filled",
            "tile_T_psum", "tile_T_done", "gemm1_psum", "silu_done", "hidden_done", "hT_psum", "hT_done",
            "gemm2_psum", "tile_out_done", "sum_done", "out_done", "apart",
        )}
        scattered = [sem(f"scattered{u}") for u in range(QUAD)]
        tile_loaded = [sem(f"tile_loaded{u}") for u in range(RING)]
        tile_scattered = [sem(f"tile_scattered{u}") for u in range(RING)]
        pair_loaded = [sem(f"pair_loaded{u}") for u in range(PAIRS)]

        def wait_apart(eng, semaphore, count):
            if static(count) and count <= 0:
                return
            eng.wait_ge(semaphore, count)
            eng.sem_inc(s["apart"], 1)

        def cols(tensor, g, width=D):
            return tensor[:, g * width:(g + 1) * width] if static(g) else tensor[:, bass.ds(g * width, width)]

        def live(g):
            return not static(g) or 0 <= g < G

        def upto(count, most=G):
            return min(count, most) if static(count) else count

        def run_steps(eng, step):
            for t in range(T_FIRST, T_LOOP):
                step(t, t % QUAD)
            with eng.Fori(T_LOOP, T_LOOP_END - QUAD + 1, QUAD) as t:
                for k in range(QUAD):
                    step(t + k, (T_LOOP + k) % QUAD)
            for t in range(T_LOOP_END, T_LAST + 1):
                step(t, t % QUAD)

        def run_tiles(eng, tile_step, lap=RING):
            first, last = -2, NT + 2
            start = TILE_LOOP
            end = start + (NT - 2 - start) // lap * lap
            for t in range(first, start):
                tile_step(t, t % lap)
            with eng.Fori(start, end - lap + 1, lap) as t:
                for k in range(lap):
                    tile_step(t + k, (start + k) % lap)
            for t in range(end, last):
                tile_step(t, t % lap)

        SCATTER_STEPS = {3: (11, (0,)), 0: (12, (1,)), 1: (13, (2, 3)), 2: (0, ())}

        def quad_of(t, offset):
            if static(t):
                q = (t - offset) // QUAD
                return q if 0 <= q < G // QUAD else None
            return t

        def quad_count(t, offset, each=1):
            if static(t):
                return each * ((t - offset) // QUAD + 1)
            return (t - (offset - QUAD)) * each // QUAD if each % QUAD else (t - (offset - QUAD)) * (each // QUAD)

        block = ctx.enter_context(nc.Block())

        @block.sync
        def _(sp):
            x_v = x.rearrange("g n d -> n g d")
            adj_v = adj.rearrange("g n m -> n g m")
            xa = x_all[:, :].rearrange("p (g d) -> p g d", d=D)
            aa = adj_all[:, :].rearrange("p (g d) -> p g d", d=N)
            sp.dma_start(xa[:, 0:X_FIRST, :], x_v[:, 0:X_FIRST, :]).then_inc(s["x_first_loaded"], 16)
            for dst, src in ((wq_sb, wq), (wk_sb, wk), (wv_sb, wv), (wo_sb, wo), (gw_sb, gate_w)):
                sp.dma_start(dst[:, :], src).then_inc(s["small_loaded"], 16)
            for j, src in ((0, bq), (1, bk), (2, bv)):
                sp.dma_start(bqkv[:, j:j + 1], src.rearrange("(p a) -> p a", a=1)).then_inc(s["small_loaded"], 16)
            for dst, src in ((bo_bc, bo), (gb_bc, gate_b)):
                sp.dma_start(dst[:, :], src.rearrange("(a d) -> a d", a=1).to_broadcast([P, dst.shape[1]])
                             ).then_inc(s["small_loaded"], 16)
            sp.dma_start(aa[:, 0:X_FIRST, :], adj_v[:, 0:X_FIRST, :]).then_inc(s["adj_first_loaded"], 16)
            sp.dma_start(xa[:, X_FIRST:G, :], x_v[:, X_FIRST:G, :]).then_inc(s["x_rest_loaded"], 16)
            sp.dma_start(aa[:, X_FIRST:G, :], adj_v[:, X_FIRST:G, :]).then_inc(s["adj_rest_loaded"], 16)
            w_v = w_sb[:, :].rearrange("p (e n) -> p e n", e=E)
            sp.dma_start(w_v[:, :, 0:HID], w1.rearrange("e d h -> d e h")).then_inc(s["experts_loaded"], 16)
            sp.dma_start(w_v[:, :, HID:2 * HID], w2.rearrange("e d h -> d e h")).then_inc(s["experts_loaded"], 16)
            for c in range(2):
                sp.dma_start(w_v[:, :, 2 * HID + c * D:2 * HID + (c + 1) * D],
                             w3[:, c * P:(c + 1) * P, :].rearrange("e p o -> p e o")).then_inc(s["experts_loaded"], 16)

            sp.wait_ge(s["free_i_done"], 1)
            for e in range(E):
                first = sp.value_load(next_free_i[0:1, e:e + 1], min_val=e * REGION, max_val=e * REGION + TOKENS)
                sp.dma_start(xs[bass.ds(first, P), :], fill[:, :]).then_inc(s["regions_filled"], 16)
            sp.dma_start(xs[FILL_ROW:FILL_ROW + P, :], fill[:, :]).then_inc(s["regions_filled"], 16)

            for u in range(QUAD):
                sp.wait_ge(scattered[u], 16 * TOPK * (G // QUAD))
            sp.wait_ge(s["regions_filled"], 16 * (E + 1))
            sp.wait_ge(s["table_done"], 2)

            def load_tile(t, u, first_lap):
                if not first_lap:
                    wait_apart(sp, tile_scattered[u], (t - u) * (16 // RING))
                row = sp.value_load(row_at[0:1, bass.ds(t, 1)], min_val=0, max_val=FILL_ROW)
                sp.dma_start(tile_in[:, u, :], xs[bass.ds(row, P), :]).then_inc(tile_loaded[u], 16)

            for t in range(RING):
                load_tile(t, t, True)
            with sp.Fori(RING, NT - RING + 1, RING) as t:
                for k in range(RING):
                    load_tile(t + k, k, False)

            for u in range(RING):
                sp.wait_ge(tile_scattered[u], 16 * (NT // RING))
            ys_v = ys[0:TOPK * TOKENS, :].rearrange("(c g p k) d -> c p g (k d)", g=CHUNK, p=P, k=TOPK)
            out_v = out.rearrange("(c g) n d -> c n g d", g=CHUNK)
            for c in range(min(PAIRS, NCHUNK)):
                sp.dma_start(pair_rows[:, c % PAIRS], ys_v[c]).then_inc(pair_loaded[c % PAIRS], 16)
            for c in range(NCHUNK):
                sp.wait_ge(s["out_done"], c + 1)
                if c + PAIRS < NCHUNK:
                    sp.dma_start(pair_rows[:, c % PAIRS], ys_v[c + PAIRS]).then_inc(pair_loaded[c % PAIRS], 16)
                sp.dma_start(out_v[c], xa[:, c * CHUNK:(c + 1) * CHUNK, :]).then_inc(s["sum_done"], 16)
            sp.wait_ge(s["sum_done"], 16 * NCHUNK)

        @block.gpsimd
        def _(pool):
            g_ = nc.gpsimd
            g_.memset(ident[:, :], 0.0)
            g_.memset(before_bf[:, :], 1.0)
            g_.memset(ones_bf[:, :], 1.0)
            g_.memset(head_of[:, :], 1.0)
            g_.memset(neg_half[:, :], -0.5)
            g_.memset(one[:, :], 1.0)
            g_.memset(upto16[:, :], 1.0)
            g_.memset(v_aug[:, :, :, :], 1.0)
            g_.memset(fill[:, :], 0.0)
            g_.memset(mean_var[:, :, :, :], 1.0)
            g_.iota(expert_iota[:, :], [[1, E]], base=0, channel_multiplier=0, allow_small_or_imprecise_dtypes=True)
            g_.iota(region_base[:, :], [[REGION // P, E]], base=0, channel_multiplier=0,
                    allow_small_or_imprecise_dtypes=True)
            g_.iota(tile_iota[:, :], [[1, NT]], base=0, channel_multiplier=0, allow_small_or_imprecise_dtypes=True)
            g_.iota(tile_row0[:, :], [[P, NT]], base=0, channel_multiplier=0, allow_small_or_imprecise_dtypes=True)
            g_.iota(dest[:, :, :], [[TOPK * P, QUAD], [1, TOPK]], base=0, channel_multiplier=TOPK,
                    allow_small_or_imprecise_dtypes=True).then_inc(s["const_zeroed"], 1)
            pool.wait_ge(s["const_zeroed"], 1)
            g_.affine_select(out=ident[:, :], in_=ident[:, :], compare_op=ALU.not_equal, fill=1.0, base=0,
                             pattern=[[-1, P]], channel_multiplier=1)
            g_.affine_select(out=before_bf[:, :], in_=before_bf[:, :], compare_op=ALU.is_gt, fill=0.0, base=0,
                             pattern=[[1, P]], channel_multiplier=-1)
            g_.affine_select(out=upto16[:, :], in_=upto16[:, :], compare_op=ALU.is_ge, fill=0.0, base=0,
                             pattern=[[1, E]], channel_multiplier=-1)
            g_.iota(fill[:, D + 1:D + 2].bitcast(I32), [[1, 1]], base=TOPK * TOKENS, channel_multiplier=1)
            g_.tensor_scalar(region_base[:, :], region_base[:, :], float(P), None, ALU.mult)
            g_.affine_select(out=head_of[:, :], in_=head_of[:, :], compare_op=ALU.is_ge, fill=0.0, base=0,
                             pattern=[[-HD, HEADS]], channel_multiplier=1).then_inc(s["const_zeroed"], 1)
            pool.wait_ge(s["const_zeroed"], 2)
            g_.affine_select(out=head_of[:, :], in_=head_of[:, :], compare_op=ALU.is_ge, fill=0.0, base=HD - 1,
                             pattern=[[HD, HEADS]], channel_multiplier=-1).then_inc(s["const_made"], 1)
            pool.wait_ge(s["bias_done"], 1)

            def step(t, k):
                if live(t + STATS) or live(t - 2):
                    b = (k + 1) % 2
                    if live(t + STATS):
                        wait_apart(pool, s["mv1_done"], t + STATS + 1)
                    if live(t - 2):
                        wait_apart(pool, s["mv2_done"], t - 1)
                    g_.tensor_scalar(var_eps[:, b, :], mean_var[:, b, :, 1], EPS, None, ALU.add
                                     ).then_inc(s["eps_done"], 1)
                    wait_apart(pool, s["eps_done"], t - T_FIRST + 1)
                    g_.tensor_tensor(rstd[:, b, :], var_eps[:, b, :], neg_half[:, :], ALU.pow
                                     ).then_inc(s["rstd_done"], 1)
                g = t + XT
                if live(g):
                    pool.wait_ge(s["xn_done"], g + 1)
                    g_.tensor_tensor(cols(x_all, g), cols(x_all, g), bo_bc[:, :], ALU.add).then_inc(s["x_bo_done"], 1)
                offset, us = SCATTER_STEPS[k]
                if us and quad_of(t, offset) is not None:
                    if k == 3:
                        pool.wait_ge(s["gates_done"], quad_count(t, offset))
                        pool.wait_ge(s["slot_done"], quad_count(t, offset))
                    for u in us:
                        wait_apart(pool, scattered[u], quad_count(t, offset + QUAD, 16 * TOPK))
                        g = t - offset + u if static(t) else t + (u - offset)
                        g_.tensor_copy(rows[:, u, :, D], gates[:, u, :])
                        g_.tensor_copy(rows[:, u, :, D + 1].bitcast(I32), dest[:, u, :])
                        g_.tensor_copy(slot_out[:, u, :], slot[:, u, :]).then_inc(s["rows_made"], 1)
                        wait_apart(pool, s["rows_made"], g + 1)
                        g_.tensor_scalar(dest[:, u, :], dest[:, u, :], float(QUAD * P * TOPK), None, ALU.add
                                         ).then_inc(s["dest_done"], 1)
                        wait_apart(pool, s["row_data"], g + 1)
                        for c in range(TOPK):
                            g_.indirect_dma_start(
                                out=xs, out_offset=bass.IndirectOffsetOnAxis(ap=slot_out[:, u, c:c + 1], axis=0),
                                in_=rows[:, u, c, :], in_offset=None,
                                bounds_check=FILL_ROW - 1, oob_is_err=False).then_inc(scattered[u], 16)
                        wait_apart(pool, s["dest_done"], g + 1)

            run_steps(pool, step)

            def scatter_tile(t, u):
                wait_apart(pool, s["tile_out_done"], t + 1)
                g_.indirect_dma_start(
                    out=ys, out_offset=bass.IndirectOffsetOnAxis(ap=tile_in[:, u, D + 1:D + 2].bitcast(I32), axis=0),
                    in_=tile_out[:, u, :], in_offset=None,
                    bounds_check=TOPK * TOKENS - 1, oob_is_err=False).then_inc(tile_scattered[u], 16)

            with pool.Fori(0, NT - RING + 1, RING) as t:
                for u in range(RING):
                    scatter_tile(t + u, u)

        @block.vector
        def _(dve):
            v = nc.vector
            dve.wait_ge(s["const_made"], 1)
            v.memset(q_pairs[:, :, :, :], 0.0)
            v.tensor_reduce(parity[:, :], head_of[:, :].rearrange("p (j a) -> p a j", a=2), AX.X, ALU.add
                            ).then_inc(s["parity_done"], 1)
            v.tensor_scalar(neg_ident[:, :], ident[:, :], NEG, None, ALU.mult)
            v.tensor_copy(next_free[:, :], region_base[:, :])
            dve.wait_ge(s["small_loaded"], 16 * 10)
            dve.wait_ge(s["parity_done"], 1)
            v.tensor_scalar(bk_parity[:, :], parity[:, :], bqkv[:, 1:2], None, ALU.mult)
            v.tensor_copy(bv_cols[:, :], bqkv[:, 2:3].to_broadcast([P, P]))
            v.tensor_scalar(bq_scaled[:, :], bqkv[:, 0:1], QSCALE, None, ALU.mult).then_inc(s["const_dve"], 1)
            dve.wait_ge(s["bias_psum"], 1)
            v.tensor_tensor(bo_bc[:, :], misc_bank[0][:, 0:D], bo_bc[:, :], ALU.add).then_inc(s["bias_done"], 1)
            dve.wait_ge(s["x_first_loaded"], 16)

            def mark_absent(first, last):
                v.tensor_scalar(no_edge[:, first * N:last * N], adj_all[:, first * N:last * N], 0.0, None, ALU.is_le
                                ).then_inc(s["mask_done"], 1)

            def route_top2(t):
                wait_apart(dve, s["logit_done"], t - 4)
                for u in range(QUAD):
                    v.max(top_val[:, u, :], logits[:, u, :]).then_inc(s["top_val_done"], 1)
                for u in range(QUAD):
                    wait_apart(dve, s["top_val_done"], t - 8 + u + 1)
                    v.max_index(top_idx[:, u, :], top_val[:, u, :], logits[:, u, :]).then_inc(s["top_idx_done"], 1)
                v.tensor_tensor(gap[:, :], top_val[:, :, 1], top_val[:, :, 0], ALU.subtract).then_inc(s["gap_done"], 1)

            def route_onehot(t):
                dve.wait_ge(s["top_idx_done"], t - 5)
                v.tensor_copy(top_f[:, :].rearrange("p (u c) -> p u c", c=TOPK), top_idx[:, :, 0:TOPK]
                              ).then_inc(s["top_f_done"], 1)
                dve.wait_ge(s["top_f_done"], quad_count(t, 9))
                v.tensor_tensor(onehot[:, :, :, :].rearrange("p u c e -> p (u c) e"),
                                expert_iota[:, :].unsqueeze(1).to_broadcast([P, QUAD * TOPK, E]),
                                top_f[:, :].unsqueeze(2).to_broadcast([P, QUAD * TOPK, E]), ALU.is_equal
                                ).then_inc(s["onehot_done"], 1)
                dve.wait_ge(s["onehot_done"], quad_count(t, 9))
                v.tensor_tensor(chosen[:, :, :], onehot[:, :, 0, :], onehot[:, :, 1, :], ALU.add
                                ).then_inc(s["chosen_done"], 1)

            def route_slots(t, misc):
                q = quad_count(t, 10)
                rank = misc[:, 256:256 + (QUAD + 1) * E].rearrange("p (u e) -> p u e", e=E)
                dve.wait_ge(s["rank_psum"], q)
                wait(dve, s["free_done"], quad_count(t, 10 + QUAD))
                v.tensor_tensor(place[:, :, :], rank[:, 0:QUAD, :],
                                next_free[:, :].unsqueeze(1).to_broadcast([P, QUAD, E]), ALU.add
                                ).then_inc(s["place_done"], 1)
                dve.wait_ge(s["place_done"], q)
                v.tensor_tensor(next_free[:, :], rank[:, QUAD, :], next_free[:, :], ALU.add).then_inc(s["free_done"], 1)
                for c in range(TOPK):
                    hot = v.tensor_tensor(place_hot[:, :, c, :], onehot[:, :, c, :], place[:, :, :], ALU.mult)
                hot.then_inc(s["place_hot_done"], 1)
                dve.wait_ge(s["place_hot_done"], q)
                wait(dve, s["rows_made"], (q - 1) * QUAD if static(q) else t - 10)
                with nc.allow_low_precision(reason="whole numbers below 2^24, exact in float32 and int32"):
                    v.tensor_reduce(slot[:, :, :].rearrange("p u c -> p (u c)"),
                                    place_hot[:, :, :, :].rearrange("p u c e -> p (u c) e"), AX.X, ALU.add
                                    ).then_inc(s["slot_done"], 1)
                dve.wait_ge(s["gap_exp_done"], q)
                v.tensor_scalar(gap_den[:, :], gap_exp[:, :], 1.0, None, ALU.add).then_inc(s["gap_den_done"], 1)
                dve.wait_ge(s["gap_den_done"], q)
                v.reciprocal(gates[:, :, 0], gap_den[:, :]).then_inc(s["gate1_done"], 1)
                dve.wait_ge(s["gate1_done"], q)
                v.tensor_tensor(gates[:, :, 1], gates[:, :, 0], gap_exp[:, :], ALU.mult).then_inc(s["gates_done"], 1)

            def step(t, k):
                m0, m1 = misc_bank[k % 2], misc_bank[(k + 1) % 2]
                if static(t) and t == X_FIRST - STATS:
                    dve.wait_ge(s["x_rest_loaded"], 16)
                if static(t) and t == -2:
                    dve.wait_ge(s["adj_first_loaded"], 16)
                    mark_absent(0, X_FIRST)
                if static(t) and t == X_FIRST - 2:
                    dve.wait_ge(s["adj_rest_loaded"], 16)
                    mark_absent(X_FIRST, G)

                def row_max(h):
                    dve.wait_ge(s["score_psum"], 2 * t + h + 1)
                    v.tensor_reduce(neg_max[:, k % 2, 4 * h:4 * h + 4],
                                    score_bank[2 * (k % 2) + h][:, :].rearrange("p (a n) -> p a n", a=4),
                                    AX.X, ALU.max, negate=True).then_inc(s["max_done"], 1)

                if live(t):
                    row_max(0)
                g = t + 1
                if live(g):
                    b = (k + 1) % 2
                    dve.wait_ge(s["qkv_done"], g + 1)
                    for j in range(4):
                        rows32 = slice(32 * j, 32 * j + 32)
                        spread = v.tensor_copy(q_pairs[rows32, b, j, :], qT[rows32, b, :])
                    spread.then_inc(s["q_spread"], 1)
                g = t - 1
                if live(g):
                    dve.wait_ge(s["pt_psum"], 2 * g + 1)
                    wait(dve, s["pv_psum"], 2 * (g - 1) + 1)
                    v.tensor_copy(probsT[:, 0:4, :], pt_bank[0][:, :].rearrange("p (h n) -> p h n", h=4)
                                  ).then_inc(s["pt0_done"], 1)
                g = t + APPLY
                if live(g):
                    b = (k + APPLY) % 2
                    dve.wait_ge(s["rstd_done"], t - T_FIRST)
                    wait(dve, s["xT_psum"], g - 1)
                    v.tensor_scalar(xn[:, b, :], cols(x_all, g), mean_var[:, b, 0, 0:1], rstd[:, b, 0:1],
                                    ALU.subtract, ALU.mult).then_inc(s["xn_done"], 1)
                g = t - 2
                if live(g):
                    dve.wait_ge(s["wo_psum"], g + 1)
                    dve.wait_ge(s["x_bo_done"], g + 1)
                    v.tensor_tensor(cols(x_all, g), m0[:, 0:D], cols(x_all, g), ALU.add).then_inc(s["x2_done"], 1)
                g = t + STATS
                if live(g):
                    b = (k + STATS) % 2
                    v.bn_stats(stats[:, 0, :], cols(x_all, g)).then_inc(s["stats1_done"], 1)
                    wait_apart(dve, s["stats1_done"], g + 1)
                    v.bn_aggr(mean_var[:, b, 0, :], stats[:, 0, :]).then_inc(s["mv1_done"], 1)
                g = t - 2
                if live(g):
                    wait_apart(dve, s["x2_done"], g + 1)
                    v.bn_stats(stats[:, 1, :], cols(x_all, g)).then_inc(s["stats2_done"], 1)
                    wait_apart(dve, s["stats2_done"], g + 1)
                    v.bn_aggr(mean_var[:, (k + 1) % 2, 1, :], stats[:, 1, :]).then_inc(s["mv2_done"], 1)
                if live(t):
                    row_max(1)
                if k == 0 and quad_of(t, 8) is not None:
                    if quad_of(t, 12) is not None:
                        dve.wait_ge(s["gap_exp_done"], quad_count(t, 12))
                    route_top2(t)
                if k == 1 and quad_of(t, 9) is not None:
                    route_onehot(t)
                g = t - 4
                if live(g):
                    if k == 0:
                        wait(dve, s["top_idx_done"], t - 4)
                    dve.wait_ge(s["logit_psum"], g + 1)
                    wait(dve, s["x2T_psum"], upto(t - 2))
                    if k == 2 and quad_of(t, 10) is not None:
                        dve.wait_ge(s["rank_psum"], quad_count(t, 10))
                    v.tensor_tensor(logits[:, k, :], m1[:, P:P + E], gb_bc[:, :], ALU.add).then_inc(s["logit_done"], 1)
                g = t - 3
                if live(g):
                    dve.wait_ge(s["x2T_psum"], g + 1)
                    v.tensor_copy(x2T[:, :], m1[:, 0:P]).then_inc(s["x2T_done"], 1)
                if k == 2 and quad_of(t, 10) is not None:
                    route_slots(t, m1)
                g = t - 1
                if live(g):
                    o_ps = m0[:, 0:HEADS * (HD + 1)].rearrange("p (h d) -> p h d", h=HEADS)
                    dve.wait_ge(s["pv_psum"], 2 * g + 2)
                    v.reciprocal(recip_sum[:, :], o_ps[:, :, HD]).then_inc(s["recip_done"], 1)
                    dve.wait_ge(s["recip_done"], g + 1)
                    wait(dve, s["oT_psum"], g)
                    v.tensor_tensor(o_norm[:, :].rearrange("p (h d) -> p h d", h=HEADS), o_ps[:, :, 0:HD],
                                    recip_sum[:, :].unsqueeze(2).to_broadcast([P, HEADS, HD]), ALU.mult
                                    ).then_inc(s["o_done"], 1)
                g = t - 2
                if live(g):
                    b = (k + 1) % 2
                    dve.wait_ge(s["rstd_done"], t - T_FIRST + 1)
                    wait(dve, s["x2T_psum"], g - 3)
                    wait(dve, s["x2n_kept"], g - 3)
                    v.tensor_scalar(x2n[:, (k + 2) % 4, :], cols(x_all, g), mean_var[:, b, 1, 0:1], rstd[:, b, 1:2],
                                    ALU.subtract, ALU.mult).then_inc(s["x2n_done"], 1)
            run_steps(dve, step)

            dve.wait_ge(s["free_done"], G // QUAD)
            v.tensor_copy(next_free_i[:, :], next_free[:, :]).then_inc(s["free_i_done"], 1)
            v.tensor_tensor(counts[:, :], next_free[:, :], region_base[:, :], ALU.subtract).then_inc(s["counts_done"], 1)
            dve.wait_ge(s["counts_psum"], 1)
            v.tensor_scalar(ntiles_a[:, :], misc_bank[0][0:E, 0:1], float(P - 1), None, ALU.add).then_inc(s["nt_a"], 1)
            dve.wait_ge(s["nt_a"], 1)
            v.tensor_scalar(ntiles_i[:, :], ntiles_a[:, :], P.bit_length() - 1, None, ALU.arith_shift_right
                            ).then_inc(s["nt_i"], 1)
            dve.wait_ge(s["nt_i"], 1)
            v.tensor_copy(ntiles[:, :], ntiles_i[:, :]).then_inc(s["nt_f"], 1)
            dve.wait_ge(s["nt_f"], 1)
            v.tensor_scalar(jump[:, :], ntiles[:, :], -float(P), float(REGION), ALU.mult, ALU.add
                            ).then_inc(s["jump_done"], 1)
            dve.wait_ge(s["upto_psum"], 1)
            v.tensor_copy(tiles_upto[:, :], misc_bank[1][0:E, 0:1]).then_inc(s["upto_done"], 1)
            dve.wait_ge(s["upto_done"], 1)
            v.tensor_scalar(passed[:, :], tile_iota[:, :], tiles_upto[:, :], None, ALU.is_ge
                            ).then_inc(s["passed_done"], 1)
            dve.wait_ge(s["table_psum"], 1)
            v.tensor_scalar(expert_f[:, :], misc_bank[0][0:1, 0:NT], float(E - 1), None, ALU.min)
            v.tensor_tensor(row_f[:, :], misc_bank[1][0:1, 0:NT], tile_row0[:, :], ALU.add).then_inc(s["table_f"], 1)
            dve.wait_ge(s["table_f"], 1)
            v.tensor_scalar(w_at[:, :], expert_f[:, :], float(WIDTH), None, ALU.mult).then_inc(s["table_done"], 1)
            v.tensor_scalar(row_at[:, :], row_f[:, :], float(FILL_ROW), None, ALU.min).then_inc(s["table_done"], 1)

            def tile_step(t, k):
                if not static(t) or 0 <= t < NT:
                    b = k % 2
                    dve.wait_ge(s["silu_done"], t + 1)
                    wait(dve, s["hT_psum"], t - 1)
                    v.tensor_tensor(hidden[:, b, :], silu[:, b, :], bank[b][:, HID:2 * HID], ALU.mult
                                    ).then_inc(s["hidden_done"], 1)
                g = t - 1
                if not static(g) or 0 <= g < NT:
                    b = (k + 1) % 2
                    dve.wait_ge(s["hT_psum"], g + 1)
                    wait(dve, s["gemm2_psum"], g - 1)
                    v.tensor_copy(hiddenT[:, b, :], bank[2 + b][:, 0:HID]).then_inc(s["hT_done"], 1)

            run_tiles(dve, tile_step)

            for c in range(NCHUNK):
                xc = x_all[:, c * CHUNK * D:(c + 1) * CHUNK * D].rearrange("p (g d) -> p g d", d=D)
                dve.wait_ge(pair_loaded[c % PAIRS], 16 * (c // PAIRS + 1))
                v.tensor_tensor(pair_sum[:, c % 2], pair_rows[:, c % PAIRS, :, 0:D], pair_rows[:, c % PAIRS, :, D:2 * D],
                                ALU.add).then_inc(s["table_f"], 1)
                dve.wait_ge(s["table_f"], c + 2)
                v.tensor_tensor(xc, xc, pair_sum[:, c % 2], ALU.add).then_inc(s["out_done"], 1)

        @block.scalar
        def _(act):
            a = nc.scalar
            act.wait_ge(s["const_dve"], 1)

            def step(t, k):
                m0, m1 = misc_bank[k % 2], misc_bank[(k + 1) % 2]

                def exps(h):
                    act.wait_ge(s["max_done"], 2 * t + h + 1)
                    wait(act, s["pt_psum"], 2 * (t - 2) + h + 1)
                    for i in range(4):
                        head = 4 * h + i
                        ex = a.activation(probs[:, k % 2, head, :], score_bank[2 * (k % 2) + h][:, i * P:(i + 1) * P],
                                          ACT.Exp, bias=neg_max[:, k % 2, head:head + 1])
                    ex.then_inc(s["exp_done"], 1)

                g = t - 2
                if live(g):
                    act.wait_ge(s["oT_psum"], g + 1)
                    a.copy(o_T[:, :], m1[:, 0:P]).then_inc(s["oT_done"], 1)
                if live(t):
                    exps(0)
                g = t - 1
                if live(g):
                    act.wait_ge(s["pt_psum"], 2 * g + 2)
                    wait(act, s["pv_psum"], 2 * (g - 1) + 2)
                    a.copy(probsT[:, 4:8, :], pt_bank[1][:, :].rearrange("p (h n) -> p h n", h=4)
                           ).then_inc(s["pt1_done"], 1)
                g = t + XT
                if live(g):
                    act.wait_ge(s["xT_psum"], g + 1)
                    wait(act, s["qkv_psum"], g - 1)
                    a.copy(xnT[:, (k + XT) % 2, :], m1[:, 0:P]).then_inc(s["xnT_done"], 1)
                if live(t):
                    exps(1)
                g = t - 3
                if live(g):
                    act.wait_ge(s["x2n_done"], g + 1)
                    a.copy(cols(x2n_all, g), x2n[:, (k + 1) % 4, :]).then_inc(s["x2n_kept"], 1)
                offset, us = SCATTER_STEPS[k]
                if us and quad_of(t, offset) is not None:
                    for u in us:
                        g = t - offset + u if static(t) else t + (u - offset)
                        act.wait_ge(s["x2n_kept"], g + 1)
                        if not static(g) or g >= QUAD:
                            act.wait_ge(scattered[u], quad_count(t, offset + QUAD, 16 * TOPK))
                        a.copy(rows[:, u, :, 0:D], cols(x2n_all, g).unsqueeze(1).to_broadcast([P, TOPK, D])
                               ).then_inc(s["row_data"], 1)
                if k == 1 and quad_of(t, 9) is not None:
                    q = quad_count(t, 9)
                    act.wait_ge(s["gap_done"], q)
                    wait(act, s["gates_done"], quad_count(t, 9 + QUAD))
                    a.activation(gap_exp[:, :], gap[:, :], ACT.Exp).then_inc(s["gap_exp_done"], 1)
                g = t + QKV
                if live(g):
                    b = (k + QKV) % 2
                    act.wait_ge(s["qkv_psum"], g + 1)
                    wait(act, s["score_psum"], 2 * (g - 2) + 2)
                    for par in range(2):
                        a.activation(k_parity[:, b, par, :], m1[:, P:2 * P], ACT.Identity,
                                     bias=bk_parity[:, par:par + 1], scale=parity[:, par:par + 1])
                    a.activation(qT[:, b, :], m1[:, 0:P], ACT.Identity, bias=bq_scaled[:, :], scale=QSCALE)
                    wait(act, s["pv_psum"], 2 * (g - 4) + 2)
                    a.copy(v_aug[:, (k + QKV) % 4, :, 0:HD], m1[:, 2 * P:3 * P].rearrange("p (h d) -> p h d", h=HEADS)
                           ).then_inc(s["qkv_done"], 1)

            run_steps(act, step)

            def tile_step(t, k):
                g = t + 1
                if not static(g) or 0 <= g < NT:
                    b = (k + 1) % 2
                    act.wait_ge(s["tile_T_psum"], g + 1)
                    wait(act, s["gemm1_psum"], g - 1)
                    a.copy(tile_T[:, b, :], bank[6 + b][:, 0:P]).then_inc(s["tile_T_done"], 1)
                if not static(t) or 0 <= t < NT:
                    b = k % 2
                    act.wait_ge(s["gemm1_psum"], t + 1)
                    wait(act, s["hidden_done"], t - 1)
                    a.activation(silu[:, b, :], bank[b][:, 0:HID], ACT.Silu).then_inc(s["silu_done"], 1)
                g = t - 2
                if not static(g) or 0 <= g < NT:
                    u = (k - 2) % RING
                    act.wait_ge(s["gemm2_psum"], g + 1)
                    if not static(g) or g >= RING:
                        act.wait_ge(tile_scattered[u], (g - u) * (16 // RING))
                    a.activation(tile_out[:, u, :], bank[4 + k % 2][:, 0:D], ACT.Copy,
                                 scale=tile_in[:, u, D:D + 1]).then_inc(s["tile_out_done"], 1)

            run_tiles(act, tile_step)

        @block.tensor
        def _(pe):
            mm, tr = nc.tensor.matmul, nc.tensor.transpose
            pe.wait_ge(s["const_dve"], 1)
            mm(misc_bank[0][:, 0:D], bv_cols[:, :], wo_sb[:, :], start=True, stop=True).then_inc(s["bias_psum"], 1)
            pe.wait_ge(s["bias_done"], 1)

            def step(t, k):
                m0, m1 = misc_bank[k % 2], misc_bank[(k + 1) % 2]

                def scores(h):
                    wait(pe, s["exp_done"], 2 * (t - 2) + h + 1)
                    at = score_bank[2 * (k % 2) + h]
                    mm(at[:, :].rearrange("p (a n) -> p a n", a=4), neg_ident[:, :],
                       cols(no_edge, t).unsqueeze(1).to_broadcast([P, 4, P]), start=True, stop=False)
                    for j in range(2):
                        last = mm(at[:, 2 * j * P:2 * (j + 1) * P], q_pairs[:, k % 2, 2 * h + j, :],
                                  k_parity[:, k % 2, :, :].rearrange("p a n -> p (a n)"), start=False, stop=(j == 1))
                    last.then_inc(s["score_psum"], 1)

                def transpose_probs(h):
                    g = t - 1
                    pe.wait_ge(s["exp_done"], 2 * g + h + 1)
                    wait(pe, s["pt1_done" if h else "pt0_done"], g)
                    for i in range(4):
                        last = tr(pt_bank[h][:, i * P:(i + 1) * P], probs[:, (k + 1) % 2, 4 * h + i, :], ident[:, :])
                    last.then_inc(s["pt_psum"], 1)

                def weigh_values(h):
                    g = t - 1
                    pe.wait_ge(s["pt1_done" if h else "pt0_done"], g + 1)
                    for head in range(4 * h, 4 * h + 4):
                        last = mm(m0[:, head * (HD + 1):(head + 1) * (HD + 1)], probsT[:, head, :],
                                  v_aug[:, (k + 3) % 4, head, :], start=True, stop=True)
                    last.then_inc(s["pv_psum"], 1)

                if live(t):
                    pe.wait_ge(s["q_spread"], t + 1)
                    if static(t):
                        pe.wait_ge(s["mask_done"], 1 if t < X_FIRST else 2)
                    scores(0)
                g = t - 2
                if live(g):
                    pe.wait_ge(s["o_done"], g + 1)
                    tr(m1[:, 0:P], o_norm[:, :], ident[:, :]).then_inc(s["oT_psum"], 1)
                if live(t - 1):
                    transpose_probs(0)
                if live(g):
                    pe.wait_ge(s["oT_done"], g + 1)
                    pe.wait_ge(s["qkv_done"], upto(t + 2))
                    if static(t):
                        wait(pe, s["x2T_done"], upto(t - 3))
                        wait(pe, s["logit_done"], upto(t - 4))
                        wait(pe, s["free_done"], upto((t - 11) // QUAD + 1, G // QUAD))
                    mm(m0[:, 0:D], o_T[:, :], wo_sb[:, :], start=True, stop=True).then_inc(s["wo_psum"], 1)
                if live(t - 1):
                    transpose_probs(1)
                g = t + XT
                if live(g):
                    pe.wait_ge(s["xn_done"], g + 1)
                    wait(pe, s["oT_done"], t - 1)
                    if static(t):
                        wait(pe, s["qkv_done"], t + 1)
                    tr(m1[:, 0:P], xn[:, (k + XT) % 2, :], ident[:, :]).then_inc(s["xT_psum"], 1)
                if live(t):
                    scores(1)
                if live(t - 1):
                    wait(pe, s["x2_done"], t - 1)
                    pe.wait_ge(s["qkv_done"], upto(t + 2))
                    weigh_values(0)
                if live(t - 4) or live(t - 3) or (k == 2 and quad_of(t, 10) is not None):
                    pe.wait_ge(s["xnT_done"], upto(t + XT + 1))
                    if static(t):
                        wait(pe, s["oT_done"], upto(t - 1))
                        wait(pe, s["x2_done"], upto(t - 2))
                        wait(pe, s["logit_done"], upto(t - 5))
                        wait(pe, s["x2T_done"], upto(t - 4))
                if live(t - 4):
                    pe.wait_ge(s["x2T_done"], t - 3)
                    mm(m1[:, P:P + E], x2T[:, :], gw_sb[:, :], start=True, stop=True).then_inc(s["logit_psum"], 1)
                if k == 2 and quad_of(t, 10) is not None:
                    pe.wait_ge(s["chosen_done"], quad_count(t, 10))
                    for u in range(QUAD + 1):
                        at = m1[:, 256 + u * E:256 + (u + 1) * E]
                        if u < QUAD:
                            last = mm(at, before_bf[:, :], chosen[:, u, :], start=True, stop=(u == 0))
                        for w in range(u):
                            last = mm(at, ones_bf[:, :], chosen[:, w, :], start=(u == QUAD and w == 0), stop=(w == u - 1))
                    last.then_inc(s["rank_psum"], 1)
                g = t - 3
                if live(g):
                    pe.wait_ge(s["x2n_done"], g + 1)
                    tr(m1[:, 0:P], x2n[:, (k + 1) % 4, :], ident[:, :]).then_inc(s["x2T_psum"], 1)
                if live(t - 1):
                    weigh_values(1)
                g = t + QKV
                if live(g):
                    b = (k + QKV) % 2
                    pe.wait_ge(s["xnT_done"], upto(g + 2))
                    wait(pe, s["x2T_done"], t - 2)
                    wait(pe, s["logit_done"], t - 3)
                    if k == 2 and quad_of(t, 10) is not None:
                        pe.wait_ge(s["free_done"], quad_count(t, 10))
                    mm(m1[:, 0:P], wq_sb[:, :], xnT[:, b, :], start=True, stop=True)
                    mm(m1[:, P:2 * P], wk_sb[:, :], xnT[:, b, :], start=True, stop=True)
                    mm(m1[:, 2 * P:3 * P], xnT[:, b, :], wv_sb[:, :], start=True, stop=True).then_inc(s["qkv_psum"], 1)

            run_steps(pe, step)

            pe.wait_ge(s["counts_done"], 1)
            mm(misc_bank[0][0:E, 0:1], counts[0:1, :], one[0:1, :], start=True, stop=True).then_inc(s["counts_psum"], 1)
            pe.wait_ge(s["nt_f"], 1)
            mm(misc_bank[1][0:E, 0:1], upto16[:, :], ntiles[:, :], start=True, stop=True).then_inc(s["upto_psum"], 1)
            pe.wait_ge(s["passed_done"], 1)
            pe.wait_ge(s["jump_done"], 1)
            mm(misc_bank[0][0:1, 0:NT], one[0:E, :], passed[:, :], start=True, stop=True)
            mm(misc_bank[1][0:1, 0:NT], jump[:, :], passed[:, :], start=True, stop=True).then_inc(s["table_psum"], 1)
            pe.wait_ge(s["table_done"], 2)
            pe.wait_ge(s["experts_loaded"], 16 * 4)

            def columns_of(t):
                return pe.value_load(w_at[0:1, bass.ds(t, 1)] if not static(t) else w_at[0:1, t:t + 1],
                                     min_val=0, max_val=(E - 1) * WIDTH)

            def due(g):
                return not static(g) or 0 <= g < NT

            columns = {}
            LAP = 2 * RING
            LAST_OF_LAP = (TILE_LOOP - 1) % LAP

            def tile_step(t, k):
                if k == (LAST_OF_LAP + 1) % LAP:
                    columns.clear()
                if due(t):
                    b = k % 2
                    col = columns[k] if k in columns else columns_of(t)
                    columns[k] = col
                    pe.wait_ge(s["tile_T_done"], t + 1)
                    wait(pe, s["hidden_done"], t - 1)
                    mm(bank[b][:, :], tile_T[:, b, :], w_sb[:, bass.ds(col, 2 * HID)], start=True, stop=True
                       ).then_inc(s["gemm1_psum"], 1)
                if due(t + 1) and k != LAST_OF_LAP:
                    columns[(k + 1) % LAP] = columns_of(t + 1)
                g = t - 2
                if due(g):
                    b = k % 2
                    col = columns.pop((k - 2) % LAP) if (k - 2) % LAP in columns else columns_of(g)
                    pe.wait_ge(s["hT_done"], g + 1)
                    wait(pe, s["tile_out_done"], g - 1)
                    for c in range(2):
                        last = mm(bank[4 + b][:, 0:D], hiddenT[:, b, c * P:(c + 1) * P],
                                  w_sb[:, bass.ds(col + (2 * HID + c * D), D)], start=(c == 0), stop=(c == 1))
                    last.then_inc(s["gemm2_psum"], 1)
                g = t + 2
                if due(g):
                    b, u = k % 2, (k + 2) % RING
                    pe.wait_ge(tile_loaded[u], (g + (RING - u)) * (16 // RING))
                    wait(pe, s["tile_T_done"], g - 1)
                    tr(bank[6 + b][:, 0:P], tile_in[:, u, 0:D], ident[:, :]).then_inc(s["tile_T_psum"], 1)
                g = t - 1
                if due(g):
                    b = (k + 1) % 2
                    pe.wait_ge(s["hidden_done"], g + 1)
                    wait(pe, s["hT_done"], g - 1)
                    for c in range(2):
                        last = tr(bank[2 + b][:, c * P:(c + 1) * P], hidden[:, b, c * P:(c + 1) * P], ident[:, :])
                    last.then_inc(s["hT_psum"], 1)

            run_tiles(pe, tile_step, LAP)


_INS = ["x", "adj", "L0_gnn_Wq", "L0_gnn_bq", "L0_gnn_Wk", "L0_gnn_bk", "L0_gnn_Wv", "L0_gnn_bv", "L0_gnn_Wo",
        "L0_gnn_bo", "L0_ffn_gate_w", "L0_ffn_gate_b", "L0_ffn_w1", "L0_ffn_w2", "L0_ffn_w3"]


def kernel(**inputs):
    import numpy as np
    import concourse.bacc as bacc
    from concourse.bass_utils import run_bass_kernel_spmd

    nc = bacc.Bacc("TRN2", target_bir_lowering=False, num_devices=1)
    arrays, args = {}, []
    for name in _INS:
        a = np.ascontiguousarray(inputs[name])
        arrays[f"in_{name}"] = a
        args.append(nc.dram_tensor(f"in_{name}", a.shape, mybir.dt.from_np(a.dtype), kind="ExternalInput").ap())
    out = nc.dram_tensor("out", arrays["in_x"].shape, F32, kind="ExternalOutput").ap()
    graph_attention_moe(nc, *args, out)
    r = run_bass_kernel_spmd(nc, [arrays], core_ids=[0])
    return r.results[0]["out"]
```

```python
from contextlib import ExitStack

import concourse.bass as bass
from concourse import mybir

F32 = mybir.dt.float32
F32R = mybir.dt.float32r
BF16 = mybir.dt.bfloat16
I32 = mybir.dt.int32
U32 = mybir.dt.uint32
ALU = mybir.AluOpType
ACT = mybir.ActivationFunctionType
AX = mybir.AxisListType

P = 128
EPS = 1e-5
NEG = -9000000000000000.0
QUAD = 4


def static(v):
    return isinstance(v, int)


def wait(eng, sem, count):
    if not static(count) or count > 0:
        eng.wait_ge(sem, count)


def graph_attention_moe(nc, x, adj, wq, bq, wk, bk, wv, bv, wo, bo, gate_w, gate_b, w1, w2, w3, out):
    G, N, D = x.shape
    E, _, HID = w1.shape
    HEADS = 8
    HD = D // HEADS
    assert N == P and D == P and HID == 2 * P and HD == 16 and G % QUAD == 0
    QSCALE = float(HD) ** -0.5
    TOKENS = G * N
    TOPK = 2
    REGION = TOKENS + P
    ROW = D + 2
    NT_MAX = TOPK * TOKENS // P + E - 1
    RING = 16
    NT = -(-NT_MAX // RING) * RING
    FILL_ROW = E * REGION
    UP, DOWN = 2 * HID, 2 * D
    CHUNK = 4
    PAIRS = 8
    LAG = 4
    TILE_LOOP = RING + LAG
    NCHUNK = G // CHUNK
    X_START, X_FIRST = 4, 12

    STATS, APPLY, XT, QKV = 5, 4, 3, 2
    T_FIRST = -STATS
    T_LOOP = 18
    T_LOOP_END = T_LOOP + (G - STATS - T_LOOP) // QUAD * QUAD
    T_LAST = G - QUAD + 9
    assert T_LOOP_END > T_LOOP

    PIECES = 64
    PIECE = E * UP // PIECES
    SPLIT_FIRST = X_FIRST - 2
    EARLY = T_LOOP - SPLIT_FIRST
    SPLIT_STEPS = EARLY + (T_LOOP_END - T_LOOP) + (PIECES - 2 * EARLY - (T_LOOP_END - T_LOOP)) // 2
    assert E * UP == G * N and UP == 2 * DOWN and EARLY > 0 and SPLIT_FIRST + SPLIT_STEPS < T_LAST
    assert (T_LOOP_END - T_LOOP) % 2 == 0 and 2 * EARLY + T_LOOP_END - T_LOOP <= PIECES

    xs = nc.dram_tensor("slots", (E * REGION + P, ROW), F32, kind="Internal").ap()
    ys = nc.dram_tensor("expert_rows", (TOPK * TOKENS, D), F32, kind="Internal").ap()

    with ExitStack() as ctx:
        def sb(name, shape, dt=F32):
            return ctx.enter_context(nc.sbuf_tensor(name, shape, dt))

        def sem(name):
            return ctx.enter_context(nc.semaphore(name))

        bank = [ctx.enter_context(nc.psum_tensor(f"bank{i}", [P, 512], F32)) for i in range(8)]
        score_bank, pt_bank, misc_bank = bank[0:4], bank[4:6], bank[6:8]

        with ExitStack() as first_use:
            adj_all = first_use.enter_context(nc.sbuf_tensor("adj_all", [P, G * N], F32))
            w12_sb = first_use.enter_context(nc.sbuf_tensor("w12_sb", [P, E * UP], F32))
        w12_hi, w12_lo = sb("w12_hi", [P, E * UP], F32R), sb("w12_lo", [P, E * UP], F32R)
        w3_sb = sb("w3_sb", [P, E * DOWN])
        no_edge = sb("no_edge", [P, G * N], BF16)
        x_all = sb("x_all", [P, G * D])
        wq_sb, wk_sb, wv_sb, wo_sb = (sb(n, [P, D]) for n in ("wq_sb", "wk_sb", "wv_sb", "wo_sb"))
        gw_sb = sb("gw_sb", [P, E])
        bo_bc, bv_cols, gb_bc = sb("bo_bc", [P, D]), sb("bv_cols", [P, P]), sb("gb_bc", [P, E])
        bqkv = sb("bqkv", [P, 3])
        ident, neg_ident = sb("ident", [P, P]), sb("neg_ident", [P, P], BF16)
        before_bf, ones_bf = sb("before_bf", [P, P], BF16), sb("ones_bf", [P, P], BF16)
        head_of, parity = sb("head_of", [P, HEADS]), sb("parity", [P, 2])
        bk_parity, bq_scaled = sb("bk_parity", [P, 2]), sb("bq_scaled", [P, 1])
        neg_half = sb("neg_half", [P, 2])
        expert_iota, region_base = sb("expert_iota", [P, E]), sb("region_base", [P, E])
        stats, mean_var = sb("stats", [P, 2, 6]), sb("mean_var", [P, 2, 2, 2])
        var_eps, rstd = sb("var_eps", [P, 2, 2]), sb("rstd", [P, 2, 2])
        xn, xnT = sb("xn", [P, 2, D]), sb("xnT", [P, 2, P])
        qT, q_pairs, k_parity = sb("qT", [P, 2, P]), sb("q_pairs", [P, 2, 4, P]), sb("k_parity", [P, 2, 2, P])
        v_aug = sb("v_aug", [P, 4, HEADS, HD + 1])
        neg_max = sb("neg_max", [P, 2, HEADS])
        probs, probsT = sb("probs", [P, 2, HEADS, P]), sb("probsT", [P, HEADS, P])
        recip_sum, o_norm, o_T = sb("recip_sum", [P, HEADS]), sb("o_norm", [P, D]), sb("o_T", [P, P])
        x2n, x2n_kept, x2T = sb("x2n", [P, 4, D]), sb("x2n_kept", [P, 16, D]), sb("x2T", [P, P])
        logits = sb("logits", [P, QUAD, E])
        top_val, top_idx = sb("top_val", [P, QUAD, 8]), sb("top_idx", [P, QUAD, 8], U32)
        top_f = sb("top_f", [P, QUAD * TOPK])
        onehot, chosen = sb("onehot", [P, QUAD, TOPK, E]), sb("chosen", [P, QUAD, E], BF16)
        gap, gap_exp, gap_den = sb("gap", [P, QUAD]), sb("gap_exp", [P, QUAD]), sb("gap_den", [P, QUAD])
        gates = sb("gates", [P, 2, QUAD, TOPK])
        next_free = sb("next_free", [P, E])
        place, place_hot = sb("place", [P, QUAD, E]), sb("place_hot", [P, QUAD, TOPK, E])
        slot = sb("slot", [P, 2, QUAD, TOPK], I32)
        slot_out = sb("slot_out", [P, QUAD, TOPK], I32)
        dest = sb("dest", [P, QUAD, TOPK])
        rows = sb("rows", [P, QUAD, TOPK, ROW])
        counts, next_free_i = sb("counts", [P, E]), sb("next_free_i", [P, E], I32)
        one = sb("one", [P, 1])
        not_behind, tile_iota, tile_row0 = sb("not_behind", [E, E]), sb("tile_iota", [E, NT]), sb("tile_row0", [1, NT])
        ntiles_a, ntiles_i = sb("ntiles_a", [E, 1], I32), sb("ntiles_i", [E, 1], I32)
        ntiles, tiles_upto, jump = sb("ntiles", [E, 1]), sb("tiles_upto", [E, 1]), sb("jump", [E, 1])
        passed = sb("passed", [E, NT])
        expert_f, row_f = sb("expert_f", [1, NT]), sb("row_f", [1, NT])
        w_at, row_at = (sb(n, [1, NT], I32) for n in ("w_at", "row_at"))
        fill = sb("fill", [P, ROW])
        tile_in = sb("tile_in", [P, RING, ROW])
        tile_T_hi, tile_T_lo = sb("tile_T_hi", [P, 2, P], F32R), sb("tile_T_lo", [P, 2, P], F32R)
        silu, hidden = (q_pairs[:, b, :, :].rearrange("p j n -> p (j n)").rearrange("p (b n) -> p b n", b=2)
                        for b in range(2))
        hiddenT = probsT[:, 0:4, :].rearrange("p h n -> p (h n)").rearrange("p (b n) -> p b n", b=2)
        tile_out = probs[:, :, :, :].rearrange("p b h n -> p (b h) n")
        pair_rows = w12_sb[:, 0:PAIRS * CHUNK * TOPK * D].rearrange("p (r g d) -> p r g d", r=PAIRS, g=CHUNK)
        pair_sum = x2n_kept[:, 0:2 * CHUNK, :].rearrange("p (r g) d -> p r g d", r=2)

        s = {n: sem(n) for n in (
            "small_loaded", "x_start_loaded", "x_first_loaded", "x_rest_loaded",
            "adj_first_loaded", "adj_rest_loaded", "experts_loaded",
            "const_zeroed", "const_made", "const_dve", "parity_done",
            "q_spread", "bias_psum", "bias_done",
            "stats1_done", "mv1_done", "eps_done", "rstd_done", "xn_done", "xT_psum", "xnT_done",
            "qkv_psum", "qkv_done", "mask_done", "score_psum", "max_done", "exp_done",
            "pt_psum", "pt0_done", "pt1_done", "pv_psum", "recip_done", "o_done", "oT_psum", "oT_done",
            "wo_psum", "x2_done", "x_bo_done", "stats2_done", "mv2_done", "x2n_done", "x2n_kept",
            "x2T_psum", "x2T_done", "logit_psum", "logit_done",
            "top_val_done", "top_idx_done", "top_f_done", "onehot_done", "chosen_done", "gap_done", "gap_exp_done",
            "rank_psum", "place_done", "free_done", "place_hot_done", "slot_done", "gap_den_done", "gate1_done",
            "gates_done", "rows_made", "row_data", "dest_done",
            "counts_done", "free_i_done", "counts_psum", "nt_a", "nt_i", "nt_f", "upto_psum", "upto_done", "jump_done",
            "passed_done", "table_psum", "table_f", "table_done", "regions_filled",
            "w12_hi_done", "w12_lo_done", "tile_T_psum", "tile_T_hi_done", "tile_T_lo_done", "gemm1_psum", "silu_done",
            "hidden_done", "hT_psum", "hT_done",
            "gemm2_psum", "tile_out_done", "pair_added", "sum_done", "out_stored", "apart",
        )}
        scattered = [sem(f"scattered{u}") for u in range(QUAD)]
        tile_loaded = [sem(f"tile_loaded{u}") for u in range(RING)]
        tile_scattered = [sem(f"tile_scattered{u}") for u in range(RING)]
        pair_loaded = [sem(f"pair_loaded{u}") for u in range(PAIRS)]

        def wait_apart(eng, semaphore, count):
            if static(count) and count <= 0:
                return
            eng.wait_ge(semaphore, count)
            eng.sem_inc(s["apart"], 1)

        def cols(tensor, g, width=D):
            return tensor[:, g * width:(g + 1) * width] if static(g) else tensor[:, bass.ds(g * width, width)]

        def kept_at(g):
            return x2n_kept[:, g % 16, :] if static(g) else x2n_kept[:, bass.ds(g % 16, 1), :].squeeze(1)

        def live(g):
            return not static(g) or 0 <= g < G

        def upto(count, most=G):
            return min(count, most) if static(count) else count

        def run_steps(eng, step):
            for t in range(T_FIRST, T_LOOP):
                step(t, t % QUAD)
            with eng.Fori(T_LOOP, T_LOOP_END - QUAD + 1, QUAD) as t:
                for k in range(QUAD):
                    step(t + k, (T_LOOP + k) % QUAD)
            for t in range(T_LOOP_END, T_LAST + 1):
                step(t, t % QUAD)

        def run_tiles(eng, tile_step):
            first, last = -2, NT + 3
            start = TILE_LOOP
            end = start + (NT - 2 - start) // RING * RING
            for t in range(first, start):
                tile_step(t, t % RING)
            with eng.Fori(start, end - RING + 1, RING) as t:
                for k in range(RING):
                    tile_step(t + k, (start + k) % RING)
            for t in range(end, last):
                tile_step(t, t % RING)

        def piece_of(t):
            if not static(t):
                return bass.ds((t - T_LOOP + 2 * EARLY) * PIECE, PIECE)
            if not 0 <= t - SPLIT_FIRST < SPLIT_STEPS:
                return None
            if t < T_LOOP:
                first = 2 * (t - SPLIT_FIRST)
            else:
                first = t - T_LOOP + 2 * EARLY + max(t - T_LOOP_END, 0)
            count = 1 if T_LOOP <= t < T_LOOP_END else 2
            return slice(first * PIECE, (first + count) * PIECE)

        def scatters(t, k):
            if static(t) and t >= G:
                return {0: (8, (0,)), 1: (9, (1, 2, 3))}.get(k, (0, ()))
            offset, us = {2: (10, (0,)), 3: (11, (1,)), 0: (12, (2,)), 1: (13, (3,))}[k]
            if static(t) and t >= G - 2:
                us = (0, 1) if k == 2 else (2, 3)
            return offset, us

        def quad_of(t, offset):
            if static(t):
                q = (t - offset) // QUAD
                return q if 0 <= q < G // QUAD else None
            return t

        def place_of(t, offset):
            return int(quad_of(t, offset) == G // QUAD - 1) if static(t) else 0

        def quad_count(t, offset, each=1):
            if static(t):
                return each * ((t - offset) // QUAD + 1)
            return (t - (offset - QUAD)) * each // QUAD if each % QUAD else (t - (offset - QUAD)) * (each // QUAD)


        block = ctx.enter_context(nc.Block())

        @block.sync
        def _(sp):
            x_v = x.rearrange("g n d -> n g d")
            adj_v = adj.rearrange("g n m -> n g m")
            xa = x_all[:, :].rearrange("p (g d) -> p g d", d=D)
            aa = adj_all[:, :].rearrange("p (g d) -> p g d", d=N)
            sp.dma_start(xa[:, 0:X_START, :], x_v[:, 0:X_START, :]).then_inc(s["x_start_loaded"], 16)
            for dst, src in ((wq_sb, wq), (wk_sb, wk), (wv_sb, wv), (wo_sb, wo), (gw_sb, gate_w)):
                sp.dma_start(dst[:, :], src).then_inc(s["small_loaded"], 16)
            for j, src in ((0, bq), (1, bk), (2, bv)):
                sp.dma_start(bqkv[:, j:j + 1], src.rearrange("(p a) -> p a", a=1)).then_inc(s["small_loaded"], 16)
            for dst, src in ((bo_bc, bo), (gb_bc, gate_b)):
                sp.dma_start(dst[:, :], src.rearrange("(a d) -> a d", a=1).to_broadcast([P, dst.shape[1]])
                             ).then_inc(s["small_loaded"], 16)
            sp.dma_start(xa[:, X_START:X_FIRST, :], x_v[:, X_START:X_FIRST, :]).then_inc(s["x_first_loaded"], 16)
            sp.dma_start(aa[:, 0:X_FIRST, :], adj_v[:, 0:X_FIRST, :]).then_inc(s["adj_first_loaded"], 16)
            sp.dma_start(xa[:, X_FIRST:G, :], x_v[:, X_FIRST:G, :]).then_inc(s["x_rest_loaded"], 16)
            sp.dma_start(aa[:, X_FIRST:G, :], adj_v[:, X_FIRST:G, :]).then_inc(s["adj_rest_loaded"], 16)
            w12_v = w12_sb[:, :].rearrange("p (e n) -> p e n", e=E)
            sp.dma_start(w12_v[:, :, 0:HID], w1.rearrange("e d h -> d e h")).then_inc(s["experts_loaded"], 16)
            sp.dma_start(w12_v[:, :, HID:UP], w2.rearrange("e d h -> d e h")).then_inc(s["experts_loaded"], 16)
            w3_v = w3_sb[:, :].rearrange("p (e n) -> p e n", e=E)
            for c in range(2):
                sp.dma_start(w3_v[:, :, c * D:(c + 1) * D],
                             w3[:, c * P:(c + 1) * P, :].rearrange("e p o -> p e o")).then_inc(s["experts_loaded"], 16)

            sp.wait_ge(s["const_made"], 1)
            sp.dma_start(xs[FILL_ROW:FILL_ROW + P, :], fill[:, :]).then_inc(s["regions_filled"], 16)
            sp.wait_ge(s["free_i_done"], 1)
            behind = [sp.alloc_register(f"behind{e}") for e in range(E)]
            sp.load(behind, next_free_i[0:1, 0:E])
            for e in range(E):
                first = sp.snap(behind[e], min_val=e * REGION, max_val=e * REGION + TOKENS)
                sp.dma_start(xs[bass.ds(first, P), :], fill[:, :]).then_inc(s["regions_filled"], 16)

            for u in range(QUAD):
                sp.wait_ge(scattered[u], 16 * TOPK * (G // QUAD))
            sp.wait_ge(s["regions_filled"], 16 * (E + 1))
            sp.wait_ge(s["table_done"], 2)

            def load_tile(t, u, first_lap):
                if not first_lap:
                    wait_apart(sp, tile_scattered[u], t - u)
                row = sp.value_load(row_at[0:1, bass.ds(t, 1)], min_val=0, max_val=FILL_ROW)
                sp.dma_start(tile_in[:, u, :], xs[bass.ds(row, P), :]).then_inc(tile_loaded[u], 16)

            for t in range(RING):
                load_tile(t, t, True)
            with sp.Fori(RING, NT - RING + 1, RING) as t:
                for k in range(RING):
                    load_tile(t + k, k, False)

            for u in range(RING):
                sp.wait_ge(tile_scattered[u], 16 * (NT // RING))
            ys_v = ys[0:TOPK * TOKENS, :].rearrange("(c g p k) d -> c p g (k d)", g=CHUNK, p=P, k=TOPK)
            out_v = out.rearrange("(c g) n d -> c n g d", g=CHUNK)
            for c in range(min(PAIRS, NCHUNK)):
                sp.dma_start(pair_rows[:, c % PAIRS], ys_v[c]).then_inc(pair_loaded[c % PAIRS], 16)
            for c in range(NCHUNK):
                sp.wait_ge(s["sum_done"], c + 1)
                if c + PAIRS < NCHUNK:
                    sp.dma_start(pair_rows[:, c % PAIRS], ys_v[c + PAIRS]).then_inc(pair_loaded[c % PAIRS], 16)
                sp.dma_start(out_v[c], xa[:, c * CHUNK:(c + 1) * CHUNK, :]).then_inc(s["out_stored"], 16)
            sp.wait_ge(s["out_stored"], 16 * NCHUNK)

        @block.gpsimd
        def _(pool):
            g_ = nc.gpsimd
            g_.memset(ident[:, :], 0.0)
            g_.memset(before_bf[:, :], 1.0)
            g_.memset(ones_bf[:, :], 1.0)
            g_.memset(head_of[:, :], 1.0)
            g_.memset(neg_half[:, :], -0.5)
            g_.memset(one[:, :], 1.0)
            g_.memset(not_behind[:, :], 1.0)
            g_.memset(v_aug[:, :, :, :], 1.0)
            g_.memset(fill[:, :], 0.0)
            g_.memset(mean_var[:, :, :, :], 1.0)
            g_.iota(expert_iota[:, :], [[1, E]], base=0, channel_multiplier=0, allow_small_or_imprecise_dtypes=True)
            g_.iota(region_base[:, :], [[REGION // P, E]], base=0, channel_multiplier=0,
                    allow_small_or_imprecise_dtypes=True)
            g_.iota(tile_iota[:, :], [[1, NT]], base=0, channel_multiplier=0, allow_small_or_imprecise_dtypes=True)
            g_.iota(tile_row0[:, :], [[P, NT]], base=0, channel_multiplier=0, allow_small_or_imprecise_dtypes=True)
            g_.iota(dest[:, :, :], [[TOPK * P, QUAD], [1, TOPK]], base=0, channel_multiplier=TOPK,
                    allow_small_or_imprecise_dtypes=True).then_inc(s["const_zeroed"], 1)
            pool.wait_ge(s["const_zeroed"], 1)
            g_.affine_select(out=ident[:, :], in_=ident[:, :], compare_op=ALU.not_equal, fill=1.0, base=0,
                             pattern=[[-1, P]], channel_multiplier=1)
            g_.affine_select(out=before_bf[:, :], in_=before_bf[:, :], compare_op=ALU.is_gt, fill=0.0, base=0,
                             pattern=[[1, P]], channel_multiplier=-1)
            g_.affine_select(out=not_behind[:, :], in_=not_behind[:, :], compare_op=ALU.is_ge, fill=0.0, base=0,
                             pattern=[[1, E]], channel_multiplier=-1)
            g_.iota(fill[:, D + 1:D + 2].bitcast(I32), [[1, 1]], base=TOPK * TOKENS, channel_multiplier=1)
            g_.tensor_scalar(region_base[:, :], region_base[:, :], float(P), None, ALU.mult)
            g_.affine_select(out=head_of[:, :], in_=head_of[:, :], compare_op=ALU.is_ge, fill=0.0, base=0,
                             pattern=[[-HD, HEADS]], channel_multiplier=1).then_inc(s["const_zeroed"], 1)
            pool.wait_ge(s["const_zeroed"], 2)
            g_.affine_select(out=head_of[:, :], in_=head_of[:, :], compare_op=ALU.is_ge, fill=0.0, base=HD - 1,
                             pattern=[[HD, HEADS]], channel_multiplier=-1).then_inc(s["const_made"], 1)

            def fill_half(t, offset, h):
                q, half = quad_count(t, offset), slice(2 * h, 2 * h + 2)
                made = 2 * q - 1 + h if static(q) else (t - 8) // 2
                if h == 0:
                    pool.wait_ge(s["gates_done"], q)
                    pool.wait_ge(s["slot_done"], q)
                    wait_apart(pool, s["dest_done"], quad_count(t, offset + QUAD))
                for u in range(half.start, half.stop):
                    wait_apart(pool, scattered[u], quad_count(t, offset + QUAD, 16 * TOPK))
                at = place_of(t, offset)
                g_.tensor_copy(rows[:, half, :, D], gates[:, at, half, :])
                g_.tensor_copy(rows[:, half, :, D + 1].bitcast(I32), dest[:, half, :])
                g_.tensor_copy(slot_out[:, half, :], slot[:, at, half, :]).then_inc(s["rows_made"], 1)
                wait_apart(pool, s["rows_made"], made)
                if h == 1:
                    g_.tensor_scalar(dest[:, :, :], dest[:, :, :], float(QUAD * P * TOPK), None, ALU.add
                                     ).then_inc(s["dest_done"], 1)

            def scatter_rows(t, offset, u):
                g = t - offset + u if static(t) else t + (u - offset)
                wait_apart(pool, s["row_data"], g + 1)
                for c in range(TOPK):
                    g_.indirect_dma_start(
                        out=xs, out_offset=bass.IndirectOffsetOnAxis(ap=slot_out[:, u, c:c + 1], axis=0),
                        in_=rows[:, u, c, :], in_offset=None,
                        bounds_check=FILL_ROW - 1, oob_is_err=False).then_inc(scattered[u], 16)

            def split_lo(t):
                piece = piece_of(t)
                wait_apart(pool, s["w12_hi_done"], t - SPLIT_FIRST + 1)
                g_.tensor_tensor(w12_lo[:, piece], w12_sb[:, piece], w12_hi[:, piece].bitcast(F32), ALU.subtract
                                ).then_inc(s["w12_lo_done"], 1)

            def step(t, k):
                if live(t + STATS) or live(t - 2):
                    b = (k + 1) % 2
                    if live(t + STATS):
                        wait_apart(pool, s["mv1_done"], t + STATS + 1)
                    if live(t - 2):
                        wait_apart(pool, s["mv2_done"], t - 1)
                    g_.tensor_scalar(var_eps[:, b, :], mean_var[:, b, :, 1], EPS, None, ALU.add
                                     ).then_inc(s["eps_done"], 1)
                    wait_apart(pool, s["eps_done"], t - T_FIRST + 1)
                    g_.tensor_tensor(rstd[:, b, :], var_eps[:, b, :], neg_half[:, :], ALU.pow
                                     ).then_inc(s["rstd_done"], 1)
                g = t + XT
                if live(g):
                    if static(t) and g == 0:
                        pool.wait_ge(s["bias_done"], 1)
                    pool.wait_ge(s["xn_done"], g + 1)
                    g_.tensor_tensor(cols(x_all, g), cols(x_all, g), bo_bc[:, :], ALU.add).then_inc(s["x_bo_done"], 1)
                offset, us = scatters(t, k)
                if quad_of(t, offset) is not None:
                    for u in us:
                        if u % 2 == 0:
                            fill_half(t, offset, u // 2)
                        scatter_rows(t, offset, u)
                if piece_of(t) is not None:
                    split_lo(t)

            run_steps(pool, step)

            def scatter_tile(t, u):
                wait_apart(pool, s["tile_out_done"], t + 1)
                g_.indirect_dma_start(
                    out=ys, out_offset=bass.IndirectOffsetOnAxis(ap=tile_in[:, u, D + 1:D + 2].bitcast(I32), axis=0),
                    in_=tile_out[:, u, :], in_offset=None,
                    bounds_check=TOPK * TOKENS - 1, oob_is_err=False).then_inc(tile_scattered[u], 16)

            with pool.Fori(0, NT - RING + 1, RING) as t:
                for u in range(RING):
                    scatter_tile(t + u, u)

        @block.vector
        def _(dve):
            v = nc.vector
            v.memset(q_pairs[:, :, :, :], 0.0)
            dve.wait_ge(s["const_made"], 1)
            v.tensor_reduce(parity[:, :], head_of[:, :].rearrange("p (j a) -> p a j", a=2), AX.X, ALU.add
                            ).then_inc(s["parity_done"], 1)
            v.tensor_scalar(neg_ident[:, :], ident[:, :], NEG, None, ALU.mult)
            v.tensor_copy(next_free[:, :], region_base[:, :])

            def mark_absent(first, last):
                v.tensor_scalar(no_edge[:, first * N:last * N], adj_all[:, first * N:last * N], 0.0, None, ALU.is_le
                                ).then_inc(s["mask_done"], 1)

            def route_top2(t, k):
                wait_apart(dve, s["logit_done"], t - 3)
                v.max(top_val[:, k, :], logits[:, k, :]).then_inc(s["top_val_done"], 1)
                wait_apart(dve, s["top_val_done"], t - 3)
                v.max_index(top_idx[:, k, :], top_val[:, k, :], logits[:, k, :]).then_inc(s["top_idx_done"], 1)
                if k == 3:
                    if quad_of(t, 11) is not None:
                        dve.wait_ge(s["gap_exp_done"], quad_count(t, 11))
                    v.tensor_tensor(gap[:, :], top_val[:, :, 1], top_val[:, :, 0], ALU.subtract
                                    ).then_inc(s["gap_done"], 1)

            def route_onehot(t):
                dve.wait_ge(s["top_idx_done"], t - 3)
                v.tensor_copy(top_f[:, :].rearrange("p (u c) -> p u c", c=TOPK), top_idx[:, :, 0:TOPK]
                              ).then_inc(s["top_f_done"], 1)
                dve.wait_ge(s["top_f_done"], quad_count(t, 7))
                v.tensor_tensor(onehot[:, :, :, :].rearrange("p u c e -> p (u c) e"),
                                expert_iota[:, :].unsqueeze(1).to_broadcast([P, QUAD * TOPK, E]),
                                top_f[:, :].unsqueeze(2).to_broadcast([P, QUAD * TOPK, E]), ALU.is_equal
                                ).then_inc(s["onehot_done"], 1)
                dve.wait_ge(s["onehot_done"], quad_count(t, 7))
                v.tensor_tensor(chosen[:, :, :], onehot[:, :, 0, :], onehot[:, :, 1, :], ALU.add
                                ).then_inc(s["chosen_done"], 1)

            def route_places(t, misc):
                q = quad_count(t, 8)
                rank = misc[:, 256:256 + (QUAD + 1) * E].rearrange("p (u e) -> p u e", e=E)
                dve.wait_ge(s["rank_psum"], q)
                wait(dve, s["free_done"], quad_count(t, 8 + QUAD))
                v.tensor_tensor(place[:, :, :], rank[:, 0:QUAD, :],
                                next_free[:, :].unsqueeze(1).to_broadcast([P, QUAD, E]), ALU.add
                                ).then_inc(s["place_done"], 1)
                dve.wait_ge(s["place_done"], q)
                v.tensor_tensor(next_free[:, :], rank[:, QUAD, :], next_free[:, :], ALU.add).then_inc(s["free_done"], 1)

            def route_slots(t, offset):
                q = quad_count(t, offset)
                for c in range(TOPK):
                    hot = v.tensor_tensor(place_hot[:, :, c, :], onehot[:, :, c, :], place[:, :, :], ALU.mult)
                hot.then_inc(s["place_hot_done"], 1)
                dve.wait_ge(s["place_hot_done"], q)
                at = place_of(t, offset)
                if not at:
                    wait(dve, s["rows_made"], quad_count(t, offset + QUAD, 2))
                with nc.allow_low_precision(reason="whole numbers below 2^24, exact in float32 and int32"):
                    v.tensor_reduce(slot[:, at, :, :].rearrange("p u c -> p (u c)"),
                                    place_hot[:, :, :, :].rearrange("p u c e -> p (u c) e"), AX.X, ALU.add
                                    ).then_inc(s["slot_done"], 1)

            def route_gates(t, offset):
                q = quad_count(t, offset)
                at = place_of(t, offset)
                if not at:
                    wait(dve, s["rows_made"], quad_count(t, offset + QUAD, 2))
                dve.wait_ge(s["gap_exp_done"], q)
                v.tensor_scalar(gap_den[:, :], gap_exp[:, :], 1.0, None, ALU.add).then_inc(s["gap_den_done"], 1)
                dve.wait_ge(s["gap_den_done"], q)
                v.reciprocal(gates[:, at, :, 0], gap_den[:, :]).then_inc(s["gate1_done"], 1)
                dve.wait_ge(s["gate1_done"], q)
                v.tensor_tensor(gates[:, at, :, 1], gates[:, at, :, 0], gap_exp[:, :], ALU.mult).then_inc(s["gates_done"], 1)

            def step(t, k):
                m0, m1 = misc_bank[k % 2], misc_bank[(k + 1) % 2]
                if static(t) and t == -STATS:
                    dve.wait_ge(s["x_start_loaded"], 16)
                if static(t) and t == X_START - STATS:
                    dve.wait_ge(s["x_first_loaded"], 16)
                if static(t) and t == X_FIRST - STATS:
                    dve.wait_ge(s["x_rest_loaded"], 16)
                if static(t) and t == -XT:
                    dve.wait_ge(s["small_loaded"], 16 * 10)
                    dve.wait_ge(s["parity_done"], 1)
                    v.tensor_scalar(bk_parity[:, :], parity[:, :], bqkv[:, 1:2], None, ALU.mult)
                    v.tensor_copy(bv_cols[:, :], bqkv[:, 2:3].to_broadcast([P, P]))
                    v.tensor_scalar(bq_scaled[:, :], bqkv[:, 0:1], QSCALE, None, ALU.mult).then_inc(s["const_dve"], 1)
                if static(t) and t == -QKV:
                    dve.wait_ge(s["bias_psum"], 1)
                    v.tensor_tensor(bo_bc[:, :], bank[0][:, 0:D], bo_bc[:, :], ALU.add).then_inc(s["bias_done"], 1)
                if static(t) and t == X_FIRST - 2:
                    dve.wait_ge(s["adj_rest_loaded"], 16)
                    mark_absent(X_FIRST, G)

                def row_max(h):
                    dve.wait_ge(s["score_psum"], 2 * t + h + 1)
                    v.tensor_reduce(neg_max[:, k % 2, 4 * h:4 * h + 4],
                                    score_bank[2 * (k % 2) + h][:, :].rearrange("p (a n) -> p a n", a=4),
                                    AX.X, ALU.max, negate=True).then_inc(s["max_done"], 1)

                g = t - 1
                if live(g):
                    dve.wait_ge(s["pt_psum"], 2 * g + 1)
                    wait(dve, s["pv_psum"], 2 * (g - 1) + 1)
                    v.tensor_copy(probsT[:, 0:4, :], pt_bank[0][:, :].rearrange("p (h n) -> p h n", h=4)
                                  ).then_inc(s["pt0_done"], 1)
                if live(t):
                    row_max(0)
                g = t - 2
                if live(g):
                    dve.wait_ge(s["wo_psum"], g + 1)
                    dve.wait_ge(s["x_bo_done"], g + 1)
                    v.tensor_tensor(cols(x_all, g), m0[:, 0:D], cols(x_all, g), ALU.add).then_inc(s["x2_done"], 1)
                g = t + STATS
                if live(g):
                    b = (k + STATS) % 2
                    wait_apart(dve, s["mv1_done"], g)
                    v.bn_stats(stats[:, 0, :], cols(x_all, g)).then_inc(s["stats1_done"], 1)
                if live(t - 2):
                    wait_apart(dve, s["x2_done"], t - 1)
                    v.bn_stats(stats[:, 1, :], cols(x_all, t - 2)).then_inc(s["stats2_done"], 1)
                if live(g):
                    wait_apart(dve, s["stats1_done"], g + 1)
                    v.bn_aggr(mean_var[:, b, 0, :], stats[:, 0, :]).then_inc(s["mv1_done"], 1)
                g = t - 2
                if live(g):
                    wait_apart(dve, s["stats2_done"], g + 1)
                    v.bn_aggr(mean_var[:, (k + 1) % 2, 1, :], stats[:, 1, :]).then_inc(s["mv2_done"], 1)
                g = t + APPLY
                if live(g):
                    b = (k + APPLY) % 2
                    dve.wait_ge(s["rstd_done"], t - T_FIRST)
                    wait(dve, s["xT_psum"], g - 1)
                    v.tensor_scalar(xn[:, b, :], cols(x_all, g), mean_var[:, b, 0, 0:1], rstd[:, b, 0:1],
                                    ALU.subtract, ALU.mult).then_inc(s["xn_done"], 1)
                if live(t):
                    row_max(1)
                g = t - 4
                if live(g):
                    dve.wait_ge(s["logit_psum"], g + 1)
                    wait(dve, s["x2T_psum"], upto(t - 2))
                    v.tensor_tensor(logits[:, k, :], m1[:, P:P + E], gb_bc[:, :], ALU.add).then_inc(s["logit_done"], 1)
                g = t - 3
                if live(g):
                    dve.wait_ge(s["x2T_psum"], g + 1)
                    v.tensor_copy(x2T[:, :], m1[:, 0:P]).then_inc(s["x2T_done"], 1)
                g = t + 1
                if live(g):
                    b = (k + 1) % 2
                    dve.wait_ge(s["qkv_done"], g + 1)
                    for j in range(4):
                        rows32 = slice(32 * j, 32 * j + 32)
                        spread = v.tensor_copy(q_pairs[rows32, b, j, :], qT[rows32, b, :])
                    spread.then_inc(s["q_spread"], 1)
                if static(t) and t == -1:
                    dve.wait_ge(s["adj_first_loaded"], 16)
                    mark_absent(0, X_FIRST)
                if live(t - 4):
                    route_top2(t, k)
                if k == 3 and quad_of(t, 7) is not None:
                    route_onehot(t)
                if not (static(t) and t >= G):
                    if k == 1 and quad_of(t, 9) is not None:
                        route_gates(t, 9)
                    if k == 2 and quad_of(t, 10) is not None:
                        route_slots(t, 10)
                if live(t - 1):
                    dve.wait_ge(s["pv_psum"], 2 * t)
                if k == 0 and quad_of(t, 8) is not None:
                    route_places(t, m0)
                g = t - 1
                if live(g):
                    o_ps = m0[:, 0:HEADS * (HD + 1)].rearrange("p (h d) -> p h d", h=HEADS)
                    v.reciprocal(recip_sum[:, :], o_ps[:, :, HD]).then_inc(s["recip_done"], 1)
                    dve.wait_ge(s["recip_done"], g + 1)
                    wait(dve, s["oT_psum"], g)
                    v.tensor_tensor(o_norm[:, :].rearrange("p (h d) -> p h d", h=HEADS), o_ps[:, :, 0:HD],
                                    recip_sum[:, :].unsqueeze(2).to_broadcast([P, HEADS, HD]), ALU.mult
                                    ).then_inc(s["o_done"], 1)
                g = t - 2
                if live(g):
                    b = (k + 1) % 2
                    dve.wait_ge(s["rstd_done"], t - T_FIRST + 1)
                    wait(dve, s["x2T_psum"], g - 3)
                    wait(dve, s["x2n_kept"], g - 3)
                    v.tensor_scalar(x2n[:, (k + 2) % 4, :], cols(x_all, g), mean_var[:, b, 1, 0:1], rstd[:, b, 1:2],
                                    ALU.subtract, ALU.mult).then_inc(s["x2n_done"], 1)
                if static(t) and t >= G and k == 0 and quad_of(t, 8) is not None:
                    route_gates(t, 8)
                    route_slots(t, 8)

            run_steps(dve, step)

            dve.wait_ge(s["free_done"], G // QUAD)
            v.tensor_copy(next_free_i[:, :], next_free[:, :]).then_inc(s["free_i_done"], 1)
            v.tensor_tensor(counts[:, :], next_free[:, :], region_base[:, :], ALU.subtract).then_inc(s["counts_done"], 1)
            dve.wait_ge(s["counts_psum"], 1)
            v.tensor_scalar(ntiles_a[:, :], misc_bank[0][0:E, 0:1], float(P - 1), None, ALU.add).then_inc(s["nt_a"], 1)
            dve.wait_ge(s["nt_a"], 1)
            v.tensor_scalar(ntiles_i[:, :], ntiles_a[:, :], P.bit_length() - 1, None, ALU.arith_shift_right
                            ).then_inc(s["nt_i"], 1)
            dve.wait_ge(s["nt_i"], 1)
            v.tensor_copy(ntiles[:, :], ntiles_i[:, :]).then_inc(s["nt_f"], 1)
            dve.wait_ge(s["nt_f"], 1)
            v.tensor_scalar(jump[:, :], ntiles[:, :], -float(P), float(REGION), ALU.mult, ALU.add
                            ).then_inc(s["jump_done"], 1)
            dve.wait_ge(s["upto_psum"], 1)
            v.tensor_copy(tiles_upto[:, :], misc_bank[1][0:E, 0:1]).then_inc(s["upto_done"], 1)
            dve.wait_ge(s["upto_done"], 1)
            v.tensor_scalar(passed[:, :], tile_iota[:, :], tiles_upto[:, :], None, ALU.is_ge
                            ).then_inc(s["passed_done"], 1)
            dve.wait_ge(s["table_psum"], 1)
            v.tensor_scalar(expert_f[:, :], misc_bank[0][0:1, 0:NT], float(E - 1), None, ALU.min)
            v.tensor_tensor(row_f[:, :], misc_bank[1][0:1, 0:NT], tile_row0[:, :], ALU.add).then_inc(s["table_f"], 1)
            dve.wait_ge(s["table_f"], 1)
            v.tensor_scalar(w_at[:, :], expert_f[:, :], float(DOWN), None, ALU.mult).then_inc(s["table_done"], 1)
            v.tensor_scalar(row_at[:, :], row_f[:, :], float(FILL_ROW), None, ALU.min).then_inc(s["table_done"], 1)

            def tile_step(t, k):
                g = t + 1
                if not static(g) or 0 <= g < NT:
                    b = (k + 1) % 2
                    dve.wait_ge(s["tile_T_hi_done"], g + 1)
                    wait(dve, s["gemm1_psum"], g - 1)
                    v.tensor_tensor(tile_T_lo[:, b, :], bank[6 + b][:, 0:P], tile_T_hi[:, b, :].bitcast(F32),
                                    ALU.subtract).then_inc(s["tile_T_lo_done"], 1)
                if not static(t) or 0 <= t < NT:
                    b = k % 2
                    dve.wait_ge(s["silu_done"], t + 1)
                    wait(dve, s["hT_psum"], t - 1)
                    v.tensor_tensor(hidden[:, b, :], silu[:, b, :], bank[b][:, HID:2 * HID], ALU.mult
                                    ).then_inc(s["hidden_done"], 1)
                g = t - 1
                if not static(g) or 0 <= g < NT:
                    b = (k + 1) % 2
                    dve.wait_ge(s["hT_psum"], g + 1)
                    wait(dve, s["gemm2_psum"], g - 1)
                    v.tensor_copy(hiddenT[:, b, :], bank[2 + b][:, 0:HID]).then_inc(s["hT_done"], 1)

            run_tiles(dve, tile_step)

            for c in range(NCHUNK):
                xc = x_all[:, c * CHUNK * D:(c + 1) * CHUNK * D].rearrange("p (g d) -> p g d", d=D)
                dve.wait_ge(pair_loaded[c % PAIRS], 16 * (c // PAIRS + 1))
                v.tensor_tensor(pair_sum[:, c % 2], pair_rows[:, c % PAIRS, :, 0:D], pair_rows[:, c % PAIRS, :, D:2 * D],
                                ALU.add).then_inc(s["pair_added"], 1)
                dve.wait_ge(s["pair_added"], c + 1)
                v.tensor_tensor(xc, xc, pair_sum[:, c % 2], ALU.add).then_inc(s["sum_done"], 1)

        @block.scalar
        def _(act):
            a = nc.scalar

            def step(t, k):
                m0, m1 = misc_bank[k % 2], misc_bank[(k + 1) % 2]

                def exps(h):
                    act.wait_ge(s["max_done"], 2 * t + h + 1)
                    wait(act, s["pt_psum"], 2 * (t - 2) + h + 1)
                    for i in range(4):
                        head = 4 * h + i
                        ex = a.activation(probs[:, k % 2, head, :], score_bank[2 * (k % 2) + h][:, i * P:(i + 1) * P],
                                          ACT.Exp, bias=neg_max[:, k % 2, head:head + 1])
                    ex.then_inc(s["exp_done"], 1)

                g = t - 2
                if live(g):
                    act.wait_ge(s["oT_psum"], g + 1)
                    a.copy(o_T[:, :], m1[:, 0:P]).then_inc(s["oT_done"], 1)
                g = t - 1
                if live(g):
                    act.wait_ge(s["pt_psum"], 2 * g + 2)
                    wait(act, s["pv_psum"], 2 * (g - 1) + 2)
                    a.copy(probsT[:, 4:8, :], pt_bank[1][:, :].rearrange("p (h n) -> p h n", h=4)
                           ).then_inc(s["pt1_done"], 1)
                g = t + XT
                if live(g):
                    act.wait_ge(s["xT_psum"], g + 1)
                    wait(act, s["qkv_psum"], g - 1)
                    a.copy(xnT[:, (k + XT) % 2, :], m1[:, 0:P]).then_inc(s["xnT_done"], 1)
                if live(t):
                    exps(0)
                g = t - 3
                if live(g):
                    act.wait_ge(s["x2n_done"], g + 1)
                    a.copy(kept_at(g), x2n[:, (k + 1) % 4, :]).then_inc(s["x2n_kept"], 1)
                offset, us = scatters(t, k)
                if quad_of(t, offset) is not None:
                    for u in us:
                        g = t - offset + u if static(t) else t + (u - offset)
                        act.wait_ge(s["x2n_kept"], g + 1)
                        if not static(g) or g >= QUAD:
                            act.wait_ge(scattered[u], quad_count(t, offset + QUAD, 16 * TOPK))
                        a.copy(rows[:, u, :, 0:D], kept_at(g).unsqueeze(1).to_broadcast([P, TOPK, D])
                               ).then_inc(s["row_data"], 1)
                piece = piece_of(t)
                if piece is not None:
                    if static(t) and t == SPLIT_FIRST:
                        act.wait_ge(s["experts_loaded"], 16 * 4)
                        act.wait_ge(s["mask_done"], 2)
                    a.copy(w12_hi[:, piece], w12_sb[:, piece]).then_inc(s["w12_hi_done"], 1)
                if live(t):
                    exps(1)
                if k == 0 and quad_of(t, 8) is not None:
                    q = quad_count(t, 8)
                    act.wait_ge(s["gap_done"], q)
                    wait(act, s["gates_done"], quad_count(t, 8 + QUAD))
                    a.activation(gap_exp[:, :], gap[:, :], ACT.Exp).then_inc(s["gap_exp_done"], 1)
                g = t + QKV
                if live(g):
                    b = (k + QKV) % 2
                    if static(t) and g == 0:
                        act.wait_ge(s["const_dve"], 1)
                    act.wait_ge(s["qkv_psum"], g + 1)
                    wait(act, s["score_psum"], 2 * (g - 2) + 2)
                    for par in range(2):
                        a.activation(k_parity[:, b, par, :], m1[:, P:2 * P], ACT.Identity,
                                     bias=bk_parity[:, par:par + 1], scale=parity[:, par:par + 1])
                    a.activation(qT[:, b, :], m1[:, 0:P], ACT.Identity, bias=bq_scaled[:, :], scale=QSCALE)
                    wait(act, s["pv_psum"], 2 * (g - 4) + 2)
                    a.copy(v_aug[:, (k + QKV) % 4, :, 0:HD], m1[:, 2 * P:3 * P].rearrange("p (h d) -> p h d", h=HEADS)
                           ).then_inc(s["qkv_done"], 1)

            run_steps(act, step)

            def tile_step(t, k):
                g = t + 1
                if not static(g) or 0 <= g < NT:
                    b = (k + 1) % 2
                    act.wait_ge(s["tile_T_psum"], g + 1)
                    wait(act, s["gemm1_psum"], g - 1)
                    a.copy(tile_T_hi[:, b, :], bank[6 + b][:, 0:P]).then_inc(s["tile_T_hi_done"], 1)
                if not static(t) or 0 <= t < NT:
                    b = k % 2
                    act.wait_ge(s["gemm1_psum"], t + 1)
                    wait(act, s["hidden_done"], t - 1)
                    a.activation(silu[:, b, :], bank[b][:, 0:HID], ACT.Silu).then_inc(s["silu_done"], 1)
                g = t - 3
                if not static(g) or 0 <= g < NT:
                    u = (k - 3) % RING
                    act.wait_ge(s["gemm2_psum"], g + 1)
                    if not static(g) or g >= RING:
                        act.wait_ge(tile_scattered[u], g - u)
                    a.activation(tile_out[:, u, :], bank[4 + (k + 1) % 2][:, 0:D], ACT.Copy,
                                 scale=tile_in[:, u, D:D + 1]).then_inc(s["tile_out_done"], 1)

            act.wait_ge(s["gates_done"], G // QUAD)
            a.activation(gap_exp[:, :], gap[:, :], ACT.Silu)
            run_tiles(act, tile_step)

        @block.tensor
        def _(pe):
            mm, tr = nc.tensor.matmul, nc.tensor.transpose

            def step(t, k):
                m0, m1 = misc_bank[k % 2], misc_bank[(k + 1) % 2]

                def absent_edges(h):
                    wait(pe, s["exp_done"], 2 * (t - 2) + h + 1)
                    mm(score_bank[2 * (k % 2) + h][:, :].rearrange("p (a n) -> p a n", a=4), neg_ident[:, :],
                       cols(no_edge, t).unsqueeze(1).to_broadcast([P, 4, P]), start=True, stop=False)

                def scores(h):
                    at = score_bank[2 * (k % 2) + h]
                    for j in range(2):
                        last = mm(at[:, 2 * j * P:2 * (j + 1) * P], q_pairs[:, k % 2, 2 * h + j, :],
                                  k_parity[:, k % 2, :, :].rearrange("p a n -> p (a n)"), start=False, stop=(j == 1))
                    last.then_inc(s["score_psum"], 1)

                def transpose_probs(h):
                    g = t - 1
                    pe.wait_ge(s["exp_done"], 2 * g + h + 1)
                    wait(pe, s["pt1_done" if h else "pt0_done"], g)
                    for i in range(4):
                        last = tr(pt_bank[h][:, i * P:(i + 1) * P], probs[:, (k + 1) % 2, 4 * h + i, :], ident[:, :])
                    last.then_inc(s["pt_psum"], 1)

                def weigh_values(h):
                    g = t - 1
                    pe.wait_ge(s["pt1_done" if h else "pt0_done"], g + 1)
                    for head in range(4 * h, 4 * h + 4):
                        last = mm(m0[:, head * (HD + 1):(head + 1) * (HD + 1)], probsT[:, head, :],
                                  v_aug[:, (k + 3) % 4, head, :], start=True, stop=True)
                    last.then_inc(s["pv_psum"], 1)

                if live(t):
                    pe.wait_ge(s["q_spread"], t + 1)
                    if static(t):
                        pe.wait_ge(s["mask_done"], 1 if t < X_FIRST else 2)
                        pe.wait_ge(s["bias_done"], 1)
                    absent_edges(0)
                    scores(0)
                if live(t - 1):
                    transpose_probs(0)
                g = t - 2
                if live(g):
                    pe.wait_ge(s["o_done"], g + 1)
                    tr(m1[:, 0:P], o_norm[:, :], ident[:, :]).then_inc(s["oT_psum"], 1)
                if live(t - 1):
                    transpose_probs(1)
                if live(t):
                    absent_edges(1)
                if live(g):
                    pe.wait_ge(s["oT_done"], g + 1)
                    pe.wait_ge(s["qkv_done"], upto(t + 2))
                    if static(t):
                        wait(pe, s["x2T_done"], upto(t - 3))
                        wait(pe, s["logit_done"], upto(t - 4))
                        wait(pe, s["free_done"], upto((t - 9) // QUAD + 1, G // QUAD))
                    mm(m0[:, 0:D], o_T[:, :], wo_sb[:, :], start=True, stop=True).then_inc(s["wo_psum"], 1)
                g = t + XT
                if live(g):
                    if static(t) and g == 0:
                        pe.wait_ge(s["const_made"], 1)
                    pe.wait_ge(s["xn_done"], g + 1)
                    wait(pe, s["oT_done"], t - 1)
                    if static(t):
                        wait(pe, s["qkv_done"], t + 1)
                    tr(m1[:, 0:P], xn[:, (k + XT) % 2, :], ident[:, :]).then_inc(s["xT_psum"], 1)
                if live(t):
                    scores(1)
                if live(t - 1):
                    wait(pe, s["x2_done"], t - 1)
                    pe.wait_ge(s["qkv_done"], upto(t + 2))
                    weigh_values(0)
                if k == 0 and quad_of(t, 8) is not None:
                    pe.wait_ge(s["chosen_done"], quad_count(t, 8))
                    pe.wait_ge(s["x2_done"], upto(t - 1))
                    if static(t):
                        pe.wait_ge(s["logit_done"], upto(t - 4))
                        pe.wait_ge(s["x2T_done"], upto(t - 3))
                    for u in range(QUAD + 1):
                        at = m0[:, 256 + u * E:256 + (u + 1) * E]
                        if u < QUAD:
                            last = mm(at, before_bf[:, :], chosen[:, u, :], start=True, stop=(u == 0))
                        for w in range(u):
                            last = mm(at, ones_bf[:, :], chosen[:, w, :], start=(u == QUAD and w == 0), stop=(w == u - 1))
                    last.then_inc(s["rank_psum"], 1)
                if live(t - 4) or live(t - 3):
                    pe.wait_ge(s["xnT_done"], upto(t + XT + 1))
                    if static(t):
                        wait(pe, s["oT_done"], upto(t - 1))
                        wait(pe, s["x2_done"], upto(t - 2))
                        wait(pe, s["logit_done"], upto(t - 5))
                        wait(pe, s["x2T_done"], upto(t - 4))
                        wait(pe, s["free_done"], upto((t - 9) // QUAD + 1, G // QUAD))
                if live(t - 4):
                    pe.wait_ge(s["x2T_done"], t - 3)
                    mm(m1[:, P:P + E], x2T[:, :], gw_sb[:, :], start=True, stop=True).then_inc(s["logit_psum"], 1)
                g = t - 3
                if live(g):
                    pe.wait_ge(s["x2n_done"], g + 1)
                    tr(m1[:, 0:P], x2n[:, (k + 1) % 4, :], ident[:, :]).then_inc(s["x2T_psum"], 1)
                if live(t - 1):
                    weigh_values(1)
                if static(t) and t == -XT:
                    pe.wait_ge(s["const_dve"], 1)
                    mm(bank[0][:, 0:D], bv_cols[:, :], wo_sb[:, :], start=True, stop=True).then_inc(s["bias_psum"], 1)
                g = t + QKV
                if live(g):
                    b = (k + QKV) % 2
                    pe.wait_ge(s["xnT_done"], upto(g + 2))
                    wait(pe, s["x2T_done"], t - 2)
                    wait(pe, s["logit_done"], t - 3)
                    mm(m1[:, 0:P], wq_sb[:, :], xnT[:, b, :], start=True, stop=True)
                    mm(m1[:, P:2 * P], wk_sb[:, :], xnT[:, b, :], start=True, stop=True)
                    mm(m1[:, 2 * P:3 * P], xnT[:, b, :], wv_sb[:, :], start=True, stop=True).then_inc(s["qkv_psum"], 1)

            run_steps(pe, step)

            pe.wait_ge(s["counts_done"], 1)
            mm(misc_bank[0][0:E, 0:1], counts[0:1, :], one[0:1, :], start=True, stop=True).then_inc(s["counts_psum"], 1)
            pe.wait_ge(s["nt_f"], 1)
            mm(misc_bank[1][0:E, 0:1], not_behind[:, :], ntiles[:, :], start=True, stop=True).then_inc(s["upto_psum"], 1)
            pe.wait_ge(s["passed_done"], 1)
            pe.wait_ge(s["jump_done"], 1)
            mm(misc_bank[0][0:1, 0:NT], one[0:E, :], passed[:, :], start=True, stop=True)
            mm(misc_bank[1][0:1, 0:NT], jump[:, :], passed[:, :], start=True, stop=True).then_inc(s["table_psum"], 1)
            pe.wait_ge(s["table_done"], 2)
            pe.wait_ge(s["experts_loaded"], 16 * 4)

            column_regs = [pe.alloc_register(f"columns{i}") for i in range(LAG + RING)]

            def load_columns(t):
                count = min(LAG + RING, NT - (t - LAG)) if static(t) else LAG + RING
                at = slice(t - LAG, t - LAG + count) if static(t) else bass.ds(t - LAG, count)
                pe.load(column_regs[0:count], w_at[0:1, at])

            def columns(i):
                return pe.snap(column_regs[i], min_val=0, max_val=(E - 1) * DOWN)

            def due(g):
                return not static(g) or 0 <= g < NT

            pe.wait_ge(s["w12_lo_done"], SPLIT_STEPS)

            def tile_step(t, k):
                i = (k - TILE_LOOP) % RING + LAG
                if static(t) and t < TILE_LOOP:
                    i = t
                    if t == 0:
                        load_columns(LAG)
                elif i == LAG:
                    load_columns(t)
                if due(t):
                    b = k % 2
                    col = columns(i)
                    pe.wait_ge(s["tile_T_hi_done"], t + 1)
                    wait(pe, s["hidden_done"], t - 1)
                    mm(bank[b][:, :], tile_T_hi[:, b, :], w12_hi[:, bass.ds(2 * col, UP)],
                       start=True, stop=False)
                    mm(bank[b][:, :], tile_T_hi[:, b, :], w12_lo[:, bass.ds(2 * col, UP)],
                       start=False, stop=False)
                    pe.wait_ge(s["tile_T_lo_done"], t + 1)
                    mm(bank[b][:, :], tile_T_lo[:, b, :], w12_hi[:, bass.ds(2 * col, UP)],
                       start=False, stop=True).then_inc(s["gemm1_psum"], 1)
                g = t - 3
                if due(g):
                    b, col = (k + 1) % 2, columns(i - 3)
                    pe.wait_ge(s["hT_done"], g + 1)
                    wait(pe, s["tile_out_done"], g - 1)
                    for c in range(2):
                        last = mm(bank[4 + b][:, 0:D], hiddenT[:, b, c * P:(c + 1) * P],
                                  w3_sb[:, bass.ds(col + c * D, D)], start=(c == 0), stop=(c == 1))
                    last.then_inc(s["gemm2_psum"], 1)
                g = t + 2
                if due(g):
                    b, u = k % 2, (k + 2) % RING
                    pe.wait_ge(tile_loaded[u], g + (RING - u))
                    wait(pe, s["tile_T_lo_done"], g - 1)
                    tr(bank[6 + b][:, 0:P], tile_in[:, u, 0:D], ident[:, :]).then_inc(s["tile_T_psum"], 1)
                g = t - 1
                if due(g):
                    b = (k + 1) % 2
                    pe.wait_ge(s["hidden_done"], g + 1)
                    wait(pe, s["hT_done"], g - 1)
                    for c in range(2):
                        last = tr(bank[2 + b][:, c * P:(c + 1) * P], hidden[:, b, c * P:(c + 1) * P], ident[:, :])
                    last.then_inc(s["hT_psum"], 1)

            run_tiles(pe, tile_step)


_INS = ["x", "adj", "L0_gnn_Wq", "L0_gnn_bq", "L0_gnn_Wk", "L0_gnn_bk", "L0_gnn_Wv", "L0_gnn_bv", "L0_gnn_Wo",
        "L0_gnn_bo", "L0_ffn_gate_w", "L0_ffn_gate_b", "L0_ffn_w1", "L0_ffn_w2", "L0_ffn_w3"]


def kernel(**inputs):
    import numpy as np
    import concourse.bacc as bacc
    from concourse.bass_utils import run_bass_kernel_spmd

    nc = bacc.Bacc("TRN2", target_bir_lowering=False, num_devices=1)
    arrays, args = {}, []
    for name in _INS:
        a = np.ascontiguousarray(inputs[name])
        arrays[f"in_{name}"] = a
        args.append(nc.dram_tensor(f"in_{name}", a.shape, mybir.dt.from_np(a.dtype), kind="ExternalInput").ap())
    out = nc.dram_tensor("out", arrays["in_x"].shape, F32, kind="ExternalOutput").ap()
    graph_attention_moe(nc, *args, out)
    r = run_bass_kernel_spmd(nc, [arrays], core_ids=[0])
    return r.results[0]["out"]
```
